# Optimizing a Trainium2 kernel written in Bass

```python
import numpy as np
import jax
import jax.numpy as jnp

def _softmax(x, axis=-1):
    return jax.nn.softmax(x, axis=axis)

def _gelu(x):
    return jax.nn.gelu(x, approximate=True)

def _silu(x):
    return jax.nn.silu(x)

def _sigmoid(x):
    return jax.nn.sigmoid(x)

def _layernorm(x, axis=-1, eps=1e-05):
    m = jnp.mean(x, axis=axis, keepdims=True)
    v = jnp.var(x, axis=axis, keepdims=True)
    return (x - m) / jnp.sqrt(v + eps)

def _scatter_add(tgt, idx, src, axis=0):
    return tgt.at[idx].add(src)

def _segment_sum(src, seg, n):
    return jax.ops.segment_sum(src, seg, n)
kernel_name = 'mk_lm_tower_d1_tok_ids1024_r4_90a8a2'

def setup_inputs(seed: int=0):
    np.random.seed(seed)
    _w = jnp.asarray

    def _rec_inputs():
        import jax
        import jax.numpy as jnp
        _rk = jax.random.key(seed)
        x = jax.random.randint(jax.random.fold_in(_rk, 1), (32, 512), 0, 99987, jnp.int32)
        return x
    x = _rec_inputs()

    def _L0_tok_setup():
        import jax, jax.numpy as jnp
        import numpy as np
        CUTOFFS = (0, 5000, 15000, 25000)
        EMBED_DIM = 256
        EMBED_FACTOR = 4
        BATCH, SEQ = (8, 1024)

        def _bucket_dims():
            return [int(EMBED_DIM // EMBED_FACTOR ** i) for i in range(len(CUTOFFS) - 1)]
        key = jax.random.key(seed)
        ks = jax.random.split(key, 8)
        x = jax.random.randint(ks[0], (BATCH, SEQ), 0, CUTOFFS[-1], dtype=jnp.int64)
        dims = _bucket_dims()
        inp = {'x': x}
        for i, d in enumerate(dims):
            size = CUTOFFS[i + 1] - CUTOFFS[i]
            t = jax.random.normal(ks[1 + i], (size, d), dtype=jnp.float32) * 0.02
            t = t.at[0].set(0.0)
            inp[f't{i}'] = t
            inp[f'w{i}'] = jax.random.normal(ks[4 + i], (d, EMBED_DIM), dtype=jnp.float32) * 0.02
        return inp
    _L0_tok_all = _L0_tok_setup()
    _L0_tok_in = {k: v for k, v in _L0_tok_all.items() if k in ('t0', 't1', 't2', 'w0', 'w1', 'w2')}
    del _L0_tok_all

    def _L0_attn_setup():
        import jax, jax.numpy as jnp
        import numpy as np
        N_HEAD = 16

        def _rope_cos_sin(T, D):
            half = D // 2
            i = jnp.arange(half, dtype=jnp.float32)
            alpha = 1.0 / 10000.0 ** (2.0 * i / D)
            ang = jnp.arange(T, dtype=jnp.float32)[:, None] * alpha
            return (jnp.cos(ang), jnp.sin(ang))

        def _apply_rope(t, cos, sin):
            half = t.shape[-1] // 2
            xr, xi = (t[..., :half], t[..., half:])
            return jnp.concatenate([xr * cos - xi * sin, xr * sin + xi * cos], axis=-1)
        key = jax.random.key(seed)
        ks = jax.random.split(key, 5)
        B, T, C = (4, 512, 256)
        s = 0.02
        x = jax.random.normal(ks[0], (B, T, C), jnp.float32)
        wq = jax.random.normal(ks[1], (C, C), jnp.float32) * s
        wk = jax.random.normal(ks[2], (C, C), jnp.float32) * s
        wv = jax.random.normal(ks[3], (C, C), jnp.float32) * s
        wp = jax.random.normal(ks[4], (C, C), jnp.float32) * s
        zb = jnp.zeros((C,), jnp.float32)
        return {'x': x, 'wq': wq, 'bq': zb, 'wk': wk, 'bk': zb, 'wv': wv, 'bv': zb, 'wp': wp, 'bp': zb}
    _L0_attn_all = _L0_attn_setup()
    _L0_attn_in = {k: v for k, v in _L0_attn_all.items() if k in ('wq', 'bq', 'wk', 'bk', 'wv', 'bv', 'wp', 'bp')}
    del _L0_attn_all

    def _L0_ffn_setup():
        import jax, jax.numpy as jnp
        import numpy as np
        DIM = 256

        def _reference_tuple_inner(x, W_r, W_k, W_v, mu_r, mu_k):
            B, T, C = x.shape
            x_prev = jnp.concatenate([jnp.zeros((B, 1, C), x.dtype), x[:, :-1, :]], axis=1)
            xr = mu_r * x + (1.0 - mu_r) * x_prev
            xk = mu_k * x + (1.0 - mu_k) * x_prev
            r = jax.nn.sigmoid(jnp.einsum('btc,dc->btd', xr, W_r))
            k = jnp.einsum('btc,dc->btd', xk, W_k)
            k_act = jnp.square(jax.nn.relu(k))
            out = r * jnp.einsum('btc,dc->btd', k_act, W_v)
            new_state = x[:, -1, :]
            return (out, new_state)
        key = jax.random.key(seed)
        ks = jax.random.split(key, 6)
        B, T, C = (8, 512, DIM)
        x = jax.random.normal(ks[0], (B, T, C), dtype=jnp.float32)
        s = 1.0 / np.sqrt(C)
        W_r = jax.random.uniform(ks[1], (C, C), jnp.float32, -s, s)
        W_k = jax.random.uniform(ks[2], (C, C), jnp.float32, -s, s)
        W_v = jax.random.uniform(ks[3], (C, C), jnp.float32, -s, s)
        mu_r = jax.random.uniform(ks[4], (C,), jnp.float32)
        mu_k = jax.random.uniform(ks[5], (C,), jnp.float32)
        return {'x': x, 'W_r': W_r, 'W_k': W_k, 'W_v': W_v, 'mu_r': mu_r, 'mu_k': mu_k}
    _L0_ffn_all = _L0_ffn_setup()
    _L0_ffn_in = {k: v for k, v in _L0_ffn_all.items() if k in ('W_r', 'W_k', 'W_v', 'mu_r', 'mu_k')}
    del _L0_ffn_all
    return {'x': x, 'L0_tok_t0': _L0_tok_in['t0'], 'L0_tok_t1': _L0_tok_in['t1'], 'L0_tok_t2': _L0_tok_in['t2'], 'L0_tok_w0': _L0_tok_in['w0'], 'L0_tok_w1': _L0_tok_in['w1'], 'L0_tok_w2': _L0_tok_in['w2'], 'L0_attn_wq': _L0_attn_in['wq'], 'L0_attn_bq': _L0_attn_in['bq'], 'L0_attn_wk': _L0_attn_in['wk'], 'L0_attn_bk': _L0_attn_in['bk'], 'L0_attn_wv': _L0_attn_in['wv'], 'L0_attn_bv': _L0_attn_in['bv'], 'L0_attn_wp': _L0_attn_in['wp'], 'L0_attn_bp': _L0_attn_in['bp'], 'L0_ffn_W_r': _L0_ffn_in['W_r'], 'L0_ffn_W_k': _L0_ffn_in['W_k'], 'L0_ffn_W_v': _L0_ffn_in['W_v'], 'L0_ffn_mu_r': _L0_ffn_in['mu_r'], 'L0_ffn_mu_k': _L0_ffn_in['mu_k']}

def reference(x, L0_tok_t0, L0_tok_t1, L0_tok_t2, L0_tok_w0, L0_tok_w1, L0_tok_w2, L0_attn_wq, L0_attn_bq, L0_attn_wk, L0_attn_bk, L0_attn_wv, L0_attn_bv, L0_attn_wp, L0_attn_bp, L0_ffn_W_r, L0_ffn_W_k, L0_ffn_W_v, L0_ffn_mu_r, L0_ffn_mu_k):
    import jax
    import jax.numpy as jnp

    def _L0_tok_ref(x, t0, t1, t2, w0, w1, w2):
        import jax, jax.numpy as jnp
        import numpy as np
        CUTOFFS = (0, 5000, 15000, 25000)
        EMBED_DIM = 256
        EMBED_FACTOR = 4
        BATCH, SEQ = (8, 1024)

        def _bucket_dims():
            return [int(EMBED_DIM // EMBED_FACTOR ** i) for i in range(len(CUTOFFS) - 1)]
        'x: [B, S] int ids -> [B, S, EMBED_DIM] float32.\n            For each bucket i covering [CUTOFFS[i], CUTOFFS[i+1]): local id lookup,\n            project to EMBED_DIM, scatter into output via mask (vectorized jnp.where).\n            '
        tables = (t0, t1, t2)
        weights = (w0, w1, w2)
        out = jnp.zeros(x.shape + (EMBED_DIM,), dtype=jnp.float32)
        for i in range(3):
            lo, hi = (CUTOFFS[i], CUTOFFS[i + 1])
            mask = (x >= lo) & (x < hi)
            local = jnp.clip(x - lo, 0, hi - lo - 1)
            e = tables[i][local]
            proj = jnp.einsum('bsd,de->bse', e, weights[i])
            out = out + jnp.where(mask[..., None], proj, 0.0)
        return out

    def _L0_attn_ref(x, wq, bq, wk, bk, wv, bv, wp, bp):
        import jax, jax.numpy as jnp
        import numpy as np
        N_HEAD = 16

        def _rope_cos_sin(T, D):
            half = D // 2
            i = jnp.arange(half, dtype=jnp.float32)
            alpha = 1.0 / 10000.0 ** (2.0 * i / D)
            ang = jnp.arange(T, dtype=jnp.float32)[:, None] * alpha
            return (jnp.cos(ang), jnp.sin(ang))

        def _apply_rope(t, cos, sin):
            half = t.shape[-1] // 2
            xr, xi = (t[..., :half], t[..., half:])
            return jnp.concatenate([xr * cos - xi * sin, xr * sin + xi * cos], axis=-1)
        B, T, C = x.shape
        H = N_HEAD
        D = C // H

        def heads(w, b):
            return (x @ w.T + b).reshape(B, T, H, D).transpose(0, 2, 1, 3)
        q, k, v = (heads(wq, bq), heads(wk, bk), heads(wv, bv))
        cos, sin = _rope_cos_sin(T, D)
        q = _apply_rope(q, cos, sin)
        k = _apply_rope(k, cos, sin)
        scale = 1.0 / np.sqrt(D).astype(np.float32)
        att = jnp.einsum('bhtd,bhsd->bhts', q, k) * scale
        causal = jnp.tril(jnp.ones((T, T), bool))
        att = jnp.where(causal, att, jnp.float32(-jnp.inf))
        att = jax.nn.softmax(att, axis=-1)
        y = jnp.einsum('bhts,bhsd->bhtd', att, v)
        y = y.transpose(0, 2, 1, 3).reshape(B, T, C)
        return y @ wp.T + bp

    def _L0_ffn_ref(x, W_r, W_k, W_v, mu_r, mu_k):
        import jax, jax.numpy as jnp
        import numpy as np
        DIM = 256

        def _reference_tuple_inner(x, W_r, W_k, W_v, mu_r, mu_k):
            B, T, C = x.shape
            x_prev = jnp.concatenate([jnp.zeros((B, 1, C), x.dtype), x[:, :-1, :]], axis=1)
            xr = mu_r * x + (1.0 - mu_r) * x_prev
            xk = mu_k * x + (1.0 - mu_k) * x_prev
            r = jax.nn.sigmoid(jnp.einsum('btc,dc->btd', xr, W_r))
            k = jnp.einsum('btc,dc->btd', xk, W_k)
            k_act = jnp.square(jax.nn.relu(k))
            out = r * jnp.einsum('btc,dc->btd', k_act, W_v)
            new_state = x[:, -1, :]
            return (out, new_state)
        return _reference_tuple_inner(x, W_r, W_k, W_v, mu_r, mu_k)[0]
    h = _L0_tok_ref(x, L0_tok_t0, L0_tok_t1, L0_tok_t2, L0_tok_w0, L0_tok_w1, L0_tok_w2)
    h = h + _L0_attn_ref(_layernorm(h, axis=-1), L0_attn_wq, L0_attn_bq, L0_attn_wk, L0_attn_bk, L0_attn_wv, L0_attn_bv, L0_attn_wp, L0_attn_bp)
    h = h + _L0_ffn_ref(_layernorm(h, axis=-1), L0_ffn_W_r, L0_ffn_W_k, L0_ffn_W_v, L0_ffn_mu_r, L0_ffn_mu_k)
    return h

_drawn_inputs = setup_inputs


def setup_inputs(seed=0):
    import zlib

    import numpy as np

    out = dict(_drawn_inputs(seed))
    spreads = {'L0_attn_bq': (0.0, 0.8),
     'L0_attn_bk': (0.0, 0.8),
     'L0_attn_bv': (0.0, 0.1),
     'L0_attn_bp': (0.0, 0.1)}
    factors = {'L0_tok_t2': 3.024,
     'L0_tok_w2': 3.021,
     'L0_attn_wq': 8.0,
     'L0_attn_wk': 8.0,
     'L0_ffn_mu_r': 8.0,
     'L0_ffn_mu_k': 6.319}
    for name, (base, spread) in spreads.items():
        noise = np.random.default_rng([zlib.crc32(name.encode()), seed]).standard_normal(out[name].shape)
        drawn = base * np.exp(spread * noise) if base else spread * noise
        out[name] = jnp.asarray(drawn.astype(out[name].dtype))
    for name, factor in factors.items():
        out[name] = (out[name] * factor).astype(out[name].dtype)
    return out
```

```python
from contextlib import ExitStack

import concourse.bass as bass
import numpy as np
from concourse import mybir

ALU = mybir.AluOpType
ACT = mybir.ActivationFunctionType
AX = mybir.AxisListType
F32, F32R, BF16, I32, U32 = (mybir.dt.float32, mybir.dt.float32r, mybir.dt.bfloat16, mybir.dt.int32,
                             mybir.dt.uint32)

P = 128
B, T, C, H = 32, 512, 256, 16
D = C // H
TB = T // P
KC = C // P
HG = 4
NG = H // HG
E0, E1, E2 = 256, 64, 16
EW = E0 + E1 + E2
EC = (EW + P - 1) // P
EL = EW - (EC - 1) * P
ROWS = 25000
NPART = 3
NCOMB = 6
Q_PART = (0, 1, 2, 0, 1, 0)
K_PART = (0, 0, 0, 1, 1, 2)
KS = NCOMB * D
KM = KS + 2
SCALE = float(D) ** -0.5
EPS = 1e-5
MASKED = -1e30

MAX_TILES = ([(3, (h,)) for h in range(HG)] + [(2, (h,)) for h in range(HG)]
             + [(1, (0, 1)), (1, (2, 3)), (0, (0, 1, 2, 3))])
NM = len(MAX_TILES)
EXP_TILES = [(0, (0, 1)), (0, (2, 3)), (1, (0, 1)), (1, (2, 3)), (2, (0, 1, 2, 3)), (3, (0, 1, 2, 3))]
NE = len(EXP_TILES)
EXP_TILES_UPTO = (2, 4, 5, 6)

SKELETON = ["U0", "M0", "PV2", "M1", 0, "U1", "M2", "PV3", "M3", 1, "U2", "M4", 2, "M5", "U3", "M6",
            "PV0", 3, "M7", "U4", "M8", 4, "M9", "U5", "M10", "PV1", 5, 6, 7]
FILL = [
    [["mT"], ["eT0", "xload"], ["eT1", "rc"], ["eT2", "st1", "rb"], ["x2T0", "idx"], ["x2T1", "mix0"],
     ["h0", "mix1"], ["h1", "ln1a", "ln1p"]],
    [["mT", "gather", "ln1n"], ["xT0", "mm0"], ["xT1", "rc", "mm1"], ["st2", "rb", "kk0"], ["q0", "sq0"], ["k0", "sw0"],
     ["kk1", "yn0", "sq1"], ["rp0"]],
    [["mT"], ["v0"], ["v1", "hi0", "rc"], ["r0", "tt0", "st3", "rb"], ["r1", "mi0"], ["lo0"],
     ["q1"], ["k1", "sw1"]],
    [["mT"], ["kv0", "rp1"], ["kv1", "fin", "out", "rc", "yn1"], ["pj0", "hi1", "rb", "st0"], ["pj1", "tt1", "hb"],
     ["ln2a", "mi1", "ln2p"], ["lo1"], ["ln2n"]],
]
STEPS = [[item for entry in SKELETON for item in (FILL[s][entry] if isinstance(entry, int) else [entry])]
         for s in range(NG)]
LIN_BATCH = {"eT0": 1, "eT1": 1, "eT2": 1, "h0": 1, "h1": 1, "xT0": 1, "xT1": 1, "q0": 1, "k0": 1,
             "q1": 1, "k1": 1, "v0": 1, "v1": 1, "pj0": -1, "pj1": -1, "x2T0": -2, "x2T1": -2,
             "kk0": -2, "kk1": -2, "r0": -2, "r1": -2, "kv0": -2, "kv1": -2}
BATCH = dict(LIN_BATCH, xload=2, idx=2, gather=2, ln1a=1, ln1p=1, ln1n=1, sw0=1, sw1=1, rp0=1, rp1=1,
             hi0=1, hi1=1, tt0=1, tt1=1, mi0=1, mi1=1, lo0=1, lo1=1, hb=1, st0=1, st1=0, st2=0, st3=0,
             yn0=-1, yn1=-1, ln2a=-1, ln2p=-1, ln2n=-1, mix0=-2, mix1=-2, mm0=-2, mm1=-2, sq0=-2, sq1=-2, fin=-2, out=-2)
GROUP = {"mT": -1, "rc": -3, "rb": -3, "PV0": -2, "PV1": -2, "PV2": -3, "PV3": -3}
GROUP.update({f"U{k}": -2 for k in range(NE)})
GROUP.update({f"M{k}": 0 for k in range(NM)})

FIRST_N, LAST_N = -2, B + 1
LOOP_FROM, LOOP_TO = 4, 30


def batch_ok(b):
    return 0 <= b < B


def count_lin_units():
    seen, n_units = {}, 0
    for n in range(FIRST_N, LAST_N + 1):
        for s in range(NG):
            for item in STEPS[s]:
                if item in LIN_BATCH:
                    key, ok = (item, n + LIN_BATCH[item]), batch_ok(n + LIN_BATCH[item])
                elif item == "mT":
                    g = NG * n + s - 1
                    key, ok = (item, g), 0 <= g < NG * B
                else:
                    continue
                if ok:
                    n_units += 1
                    seen[key] = n_units
    return seen


LIN = count_lin_units()


class Turn:

    def __init__(self, n=None, register=None, offset=0):
        self.register, self.offset = register, offset
        self.ns = [n] if register is None else list(range(LOOP_FROM + offset, LOOP_TO + offset, 2))
        self.parity = self.ns[0] % 2

    def has(self, item, s):
        def ok(n):
            if item in GROUP:
                return 0 <= NG * n + s + GROUP[item] < NG * B
            return batch_ok(n + BATCH[item])
        return all(ok(n) for n in self.ns)

    def at(self, count):
        if all(count(n) <= 0 for n in self.ns):
            return None
        return self.value(count)

    def value(self, count):
        vs = [count(n) for n in self.ns]
        if self.register is None:
            return vs[0]
        slope = (vs[-1] - vs[0]) // (self.ns[-1] - self.ns[0])
        assert all(v == vs[0] + slope * (n - self.ns[0]) for v, n in zip(vs, self.ns)) and vs[0] > 0
        return self.register * slope + (vs[0] - slope * (self.ns[0] - self.offset))


def turns(engine):
    for n in range(FIRST_N, LOOP_FROM):
        yield Turn(n)
    with engine.Fori(LOOP_FROM, LOOP_TO - 1, 2) as register:
        for offset in range(2):
            yield Turn(register=register, offset=offset)
    for n in range(LOOP_TO, LAST_N + 1):
        yield Turn(n)


def lin(unit, key):
    return LIN.get((unit, key), 0)


def tower(nc, ids, table, w_tok, w_qkv, b_qk, w_p, b_v, b_p, w_r, w_k, w_v, mu, cos_sin, consts, out):
    with ExitStack() as ctx:
        def sb(name, shape, dt=F32):
            return ctx.enter_context(nc.sbuf_tensor(name, shape, dt))

        def psum(name, shape):
            return ctx.enter_context(nc.psum_tensor(name, shape, F32))

        def sem(name):
            return ctx.enter_context(nc.semaphore(name))

        ps_exp = psum("ps_exp", [P, 2, 2, T])
        ps_max = psum("ps_max", [P, 2, T])
        ps_pv = psum("ps_pv", [P, T])
        ps_lin = psum("ps_lin", [P, T])

        wtok = sb("wtok", [P, EC, C])
        wqkv_hi = sb("wqkv_hi", [P, KC, 3 * C], F32R)
        wqkv_lo = sb("wqkv_lo", [P, KC, 3 * C], F32R)
        wp = sb("wp", [P, KC, C])
        wr = sb("wr", [P, KC, C])
        wk = sb("wk", [P, KC, C])
        wv = sb("wv", [P, KC, C])
        bqk = sb("bqk", [P, 4])
        bvcol = sb("bvcol", [P, KC])
        bprow = sb("bprow", [1, C])
        ones_row = sb("ones_row", [1, P])
        bias_p = sb("bias_p", [P, C])
        muc = sb("muc", [P, 2, KC])
        rope = sb("rope", [P, 2, T])
        cst = sb("cst", [P, 2, P])
        ident_bf = sb("ident_bf", [P, P], BF16)
        mask_bf = sb("mask_bf", [P, P], BF16)
        minus_half = sb("minus_half", [P, TB])
        ids_sb = sb("ids_sb", [P, TB], I32)
        row_t = sb("row_t", [P, TB], I32)
        row_id = sb("row_id", [P, TB], U32)
        emb = sb("emb", [P, TB, EW])
        embT = sb("embT", [P, EC, T])
        h = sb("h", [P, TB, C])
        xn = sb("xn", [P, TB, C])
        xT_hi = sb("xT_hi", [P, KC, T], F32R)
        xT_lo = sb("xT_lo", [P, KC, T], F32R)
        raw = sb("raw", [P, 2, T])
        swapped = sb("swapped", [P, 2, T])
        parts = [sb(f"part{j}", [P, KC, 2, T], BF16) for j in range(NPART)]
        qs = sb("qs", [KM, H, T], BF16)
        ks = sb("ks", [KM, H, T], BF16)
        vx = [sb(f"vx{p}", [P, TB, C, 2]) for p in range(2)]
        probs = [sb(f"probs{j}", [P, HG, T - P * j]) for j in range(TB)]
        rowmax = sb("rowmax", [P, 2, HG * TB])
        maxT = sb("maxT", [HG * TB, 2, 2, P], BF16)
        y_raw = sb("y_raw", [P, 2, T])
        y = [sb(f"y{p}", [P, KC, T]) for p in range(2)]
        sums = sb("sums", [P, NG, HG * T // P])
        inv_sums = sb("inv_sums", [P, NG, HG * T // P])
        inv_rows = sb("inv_rows", [P, KC, T])
        hb = [sb(f"hb{p}", [P, TB, C]) for p in range(2)]
        h1 = sb("h1", [P, TB, C])
        xn2 = sb("xn2", [P, TB, C])
        x2T = sb("x2T", [P, KC, T + 1])
        mix_r = sb("mix_r", [P, KC, T])
        mix_k = sb("mix_k", [P, KC, T])
        kact = sb("kact", [P, KC, T])
        gate = sb("gate", [P, TB, C])
        ln = [dict(stats=sb(f"ln_stats{j}", [P, TB, 6]), mv=sb(f"ln_mv{j}", [P, TB, 2]),
                   var=sb(f"ln_var{j}", [P, TB]), rstd=sb(f"ln_rstd{j}", [P, TB])) for j in range(2)]
        inv_dram = nc.dram_tensor("inv_dram", [NG, HG, T], F32, kind="Internal").ap()

        s_load = sem("s_load")
        s_setup = sem("s_setup")
        s_bias_mm = sem("s_bias_mm")
        s_ready = sem("s_ready")
        lin_full = sem("lin_full")
        lin_drained = sem("lin_drained")
        ids_in = sem("ids_in")
        rows_done = sem("rows_done")
        gathered = sem("gathered")
        ln_step = [sem(f"ln{j}_step") for j in range(2)]
        ln_rstd = [sem(f"ln{j}_rstd") for j in range(2)]
        ln_out = [sem(f"ln{j}_out") for j in range(2)]
        xT_hi_done = sem("xT_hi_done")
        swap_in = [sem(f"swap_in{c}") for c in range(KC)]
        rope_step = sem("rope_step")
        split_hi = sem("split_hi")
        split_rest = sem("split_rest")
        split_mid = sem("split_mid")
        split_lo = sem("split_lo")
        stack_in = [sem(f"stack_in{g}") for g in range(NG)]
        max_full = sem("max_full")
        max_done = sem("max_done")
        max_hi = sem("max_hi")
        max_in = [sem(f"max_in{g}") for g in range(NG)]
        exp_full = sem("exp_full")
        exp_done = sem("exp_done")
        masked = sem("masked")
        pv_done = sem("pv_done")
        y_out = sem("y_out")
        y_in = [sem(f"y_in{g}") for g in range(NG)]
        inv_done = sem("inv_done")
        inv_out = [sem(f"inv_out{g}") for g in range(NG)]
        inv_in = [sem(f"inv_in{g}") for g in range(NG)]
        y_norm = sem("y_norm")
        hb_done = sem("hb_done")
        mix_diff = sem("mix_diff")
        mix_step = sem("mix_step")
        sq_done = sem("sq_done")
        fin_done = sem("fin_done")
        stored = sem("stored")

        passed = {e: sem(f"passed_{e}") for e in ("sp", "dve", "pool")}
        NSTACK = 2 * NCOMB
        stage = probs[0].rearrange("p a b -> p (a b)")[:, 0:KC * 3 * C].rearrange("p (k c) -> p k c", k=KC)
        block = ctx.enter_context(nc.Block())

        def sync_part(sp, turn, s, item):
            if item == "xload" and turn.has(item, s):
                if (v := turn.at(lambda n: 2 * (n + 2))) is not None:
                    sp.wait_ge(rows_done, v)
                    sp.sem_inc(passed["sp"], 1)
                b = turn.value(lambda n: n + 2) if turn.register is not None else turn.ns[0] + 2
                src = ids[b] if isinstance(b, int) else ids[bass.ds(b, 1)].rearrange("a p t -> (a p) t")
                sp.dma_start(ids_sb[:], src).then_inc(ids_in, 16)
            elif item in ("sw0", "sw1") and turn.has(item, s):
                c = int(item[-1])
                if (v := turn.at(lambda n: lin(f"k{c}", n + 1))) is not None:
                    sp.wait_ge(lin_drained, v)
                    sp.sem_inc(passed["sp"], 1)
                for blk in range(4):
                    to, of = 32 * blk, 32 * (blk ^ 1)
                    sp.dma_start(swapped[to:to + 32, :, :], raw[of:of + 32, :, :]).then_inc(swap_in[c], 16)
            elif item in ("st0", "st1", "st2", "st3") and turn.has(item, s):
                g = int(item[-1])
                c, off = g // 2, BATCH[item]
                if (v := turn.at(lambda n: KC * (n + off) + c + 1)) is not None:
                    sp.wait_ge(split_lo, v)
                    sp.sem_inc(passed["sp"], 1)
                if (v := turn.at(lambda n: NM * (NG * (n + off - 1) + g + 1))) is not None:
                    sp.wait_ge(max_full, v)
                    sp.sem_inc(passed["sp"], 1)
                if (v := turn.at(lambda n: NE * (NG * (n + off - 1) + g + 1))) is not None:
                    sp.wait_ge(exp_full, v)
                    sp.sem_inc(passed["sp"], 1)
                rows = slice(64 * (g % 2), 64 * (g % 2) + 64)
                for k in range(NCOMB):
                    for j, (stack, part) in enumerate(((qs, Q_PART[k]), (ks, K_PART[k]))):
                        sp.dma_start(stack[D * k:D * k + D, HG * g:HG * g + HG, :],
                                     parts[part][rows, c, j, :]).then_inc(stack_in[g], 16)
            elif item == "mT" and turn.has(item, s):
                g = (s - 1) % NG
                if (v := turn.at(lambda n: lin("mT", NG * n + s - 1))) is not None:
                    sp.wait_ge(lin_drained, v)
                    sp.sem_inc(passed["sp"], 1)
                for j in range(2):
                    sp.dma_start(qs[KS + j:KS + j + 1, HG * g:HG * g + HG, :], maxT[:, g % 2, j, :]).then_inc(max_in[g], 16)
            elif item == "PV3" and turn.has(item, s):
                g = (s - 3) % NG
                c = g // 2
                if (v := turn.at(lambda n: NG * n + s - 3 + 1)) is not None:
                    sp.wait_ge(y_out, v)
                    sp.sem_inc(passed["sp"], 1)
                if (v := turn.at(lambda n: lin("pj1", (NG * n + s - 3) // NG - 2))) is not None:
                    sp.wait_ge(lin_full, v)
                    sp.sem_inc(passed["sp"], 1)
                par = (turn.parity + (s - 3) // NG) % 2
                sp.dma_start(y[par][64 * (g % 2):64 * (g % 2) + 64, c, :], y_raw[0:P:2, g % 2, :]).then_inc(y_in[g], 16)
                sp.dma_start(sums[:, g, :], y_raw[1:P:32, g % 2, :]).then_inc(y_in[g], 16)
            elif item == "rb" and turn.has(item, s):
                g = (s - 3) % NG
                c = g // 2
                if (v := turn.at(lambda n: NG * n + s - 3 + 1)) is not None:
                    sp.wait_ge(inv_done, v)
                    sp.sem_inc(passed["sp"], 1)
                sp.dma_start(inv_dram[g].rearrange("h (q t) -> (h q) t", t=HG * T // P), inv_sums[:, g, :]).then_inc(inv_out[g], 16)
                if (v := turn.at(lambda n: 16 * ((NG * n + s - 3) // NG + 1))) is not None:
                    sp.wait_ge(inv_out[g], v)
                    sp.sem_inc(passed["sp"], 1)
                if (v := turn.at(lambda n: KC * ((NG * n + s - 3) // NG - 1) + c + 1)) is not None:
                    sp.wait_ge(y_norm, v)
                    sp.sem_inc(passed["sp"], 1)
                sp.dma_start(inv_rows[64 * (g % 2):64 * (g % 2) + 64, c, :],
                             inv_dram[g].unsqueeze(1).to_broadcast([HG, D, T])).then_inc(inv_in[g], 16)
            elif item == "out" and turn.has(item, s):
                if (v := turn.at(lambda n: n - 2 + 1)) is not None:
                    sp.wait_ge(fin_done, v)
                    sp.sem_inc(passed["sp"], 1)
                b = turn.value(lambda n: n - 2) if turn.register is not None else turn.ns[0] - 2
                dst = out[b] if isinstance(b, int) else out[bass.ds(b, 1)].rearrange("a p k c -> (a p) k c")
                sp.dma_start(dst, gate[:]).then_inc(stored, 16)

        @block.sync
        def _(sp):
            loads = [(wtok[:, 0:EC - 1, :], w_tok[0:(EC - 1) * P, :].rearrange("(k p) c -> p k c", p=P)),
                     (wtok[0:EL, EC - 1, :], w_tok[(EC - 1) * P:EW, :]),
                     (stage, w_qkv.rearrange("(k p) c -> p k c", p=P))]
            loads += [(to, of.rearrange("(k p) c -> p k c", p=P)) for to, of in ((wp, w_p), (wr, w_r), (wk, w_k), (wv, w_v))]
            loads += [(bqk[:], b_qk), (bvcol[:], b_v), (bprow[:], b_p), (muc[:], mu), (rope[:], cos_sin), (cst[:], consts)]
            assert len(loads) == NLOADS
            for to, of in loads:
                sp.dma_start(to[:] if not isinstance(to, bass.AP) else to, of).then_inc(s_load, 16)
            sp.wait_ge(s_load, 16 * NLOADS)
            for turn in turns(sp):
                for s in range(NG):
                    for item in STEPS[s]:
                        sync_part(sp, turn, s, item)
            sp.wait_ge(stored, 16 * B)

        def lin_unit(pe, turn, s, item):
            key = (lambda n: NG * n + s - 1) if item == "mT" else (lambda n: n + LIN_BATCH[item])
            if (v := turn.at(lambda n: lin(item, key(n)) - 1)) is not None:
                pe.wait_ge(lin_drained, v)

        def tensor_part(pe, turn, s, item):
            if item[0] == "M":
                k = int(item[1:])
                tb, heads = MAX_TILES[k]
                g = s
                slot = (g + k) % 2
                if k == 0:
                    if (v := turn.at(lambda n: 16 * NSTACK * (n + 1))) is not None:
                        pe.wait_ge(stack_in[g], v)
                if (v := turn.at(lambda n: NM * (NG * n + s) + k - 1)) is not None:
                    pe.wait_ge(max_done, v)
                width = P * (tb + 1)
                tile = ps_max[:, slot, 0:width * len(heads)].rearrange("p (h t) -> p h t", h=len(heads))
                pe.matmul(tile[:, :, P * tb:], ident_bf[:], mask_bf[:].unsqueeze(1).to_broadcast([P, len(heads), P]),
                          start=True, stop=False, skip_group_check=True)
                for j, hd in enumerate(heads):
                    hh = HG * g + hd
                    mm = pe.matmul(tile[:, j, :], qs[0:KS, hh, P * tb:P * tb + P], ks[0:KS, hh, 0:width],
                                   start=False, stop=(j == len(heads) - 1), skip_group_check=True)
                mm.then_inc(max_full, 1)
            elif item[0] == "U":
                k = int(item[1:])
                sbk, heads = EXP_TILES[k]
                g = (s - 2) % NG
                slot = k % 2
                if k == 0:
                    if (v := turn.at(lambda n: 32 * ((NG * n + s - 2) // NG + 1))) is not None:
                        pe.wait_ge(max_in[g], v)
                if (v := turn.at(lambda n: NE * (NG * n + s - 2) + k - 1)) is not None:
                    pe.wait_ge(exp_done, v)
                width = T - P * sbk
                per_bank = T // width if len(heads) == 4 else 1
                for j, hd in enumerate(heads):
                    hh = HG * g + hd
                    off = width * (j % per_bank)
                    mm = pe.matmul(ps_exp[:, slot, j // per_bank, off:off + width], ks[:, hh, P * sbk:P * sbk + P],
                                   qs[:, hh, P * sbk:T], start=(j % per_bank == 0), stop=(j % per_bank == per_bank - 1),
                                   skip_group_check=True)
                mm.then_inc(exp_full, 1)
            elif item[0:2] == "PV":
                sbk = int(item[2])
                g = (s + GROUP[item]) % NG
                off = GROUP[item]
                par = (turn.parity + (s + off) // NG) % 2
                if (v := turn.at(lambda n: TB * (NG * n + s + off) + sbk + 1)) is not None:
                    pe.wait_ge(masked, v)
                if sbk == 0:
                    if (v := turn.at(lambda n: NG * n + s + off)) is not None:
                        pe.wait_ge(y_out, v)
                    if (v := turn.at(lambda n: lin("v1", (NG * n + s + off) // NG))) is not None:
                        pe.wait_ge(lin_drained, v)
                for j in range(HG):
                    hh = HG * g + j
                    mm = pe.matmul(ps_pv[32 * j:32 * j + 32, P * sbk:T],
                                   vx[par][:, sbk, D * hh:D * hh + D, :].rearrange("p d e -> p (d e)"),
                                   probs[sbk][:, j, :], start=(sbk == 0), stop=(sbk == TB - 1), skip_group_check=True)
                mm.then_inc(pv_done, 1)
            elif item == "mT":
                g = (s - 1) % NG
                lin_unit(pe, turn, s, item)
                if (v := turn.at(lambda n: NM * (NG * n + s))) is not None:
                    pe.wait_ge(max_done, v)
                pe.transpose(ps_lin[0:HG * TB, 0:P], rowmax[:, g % 2, :], cst[:, 0, :]).then_inc(lin_full, 1)
            elif item[:2] == "eT":
                c = int(item[2])
                rows = P if c < EC - 1 else EL
                lin_unit(pe, turn, s, item)
                if (v := turn.at(lambda n: 16 * TB * (n + 1 + 1))) is not None:
                    pe.wait_ge(gathered, v)
                for tb in range(TB):
                    mm = pe.transpose(ps_lin[0:rows, P * tb:P * tb + P], emb[:, tb, P * c:P * c + rows], cst[:, 0, :])
                mm.then_inc(lin_full, 1)
            elif item in ("h0", "h1"):
                u = int(item[1])
                lin_unit(pe, turn, s, item)
                if (v := turn.at(lambda n: lin("eT2", n + 1))) is not None:
                    pe.wait_ge(lin_drained, v)
                for j in range(2):
                    tb = 2 * u + j
                    for c in range(EC):
                        rows = P if c < EC - 1 else EL
                        mm = pe.matmul(ps_lin[:, C * j:C * j + C], embT[0:rows, c, P * tb:P * tb + P], wtok[0:rows, c, :],
                                       start=(c == 0), stop=(c == EC - 1))
                mm.then_inc(lin_full, 1)
            elif item[:2] == "xT" or item[:3] == "x2T":
                c = int(item[-1])
                first = item[:2] == "xT"
                off, src = (1, xn) if first else (-2, xn2)
                lin_unit(pe, turn, s, item)
                if (v := turn.at(lambda n: TB * (n + off + 1))) is not None:
                    pe.wait_ge(ln_out[0 if first else 1], v)
                for tb in range(TB):
                    mm = pe.transpose(ps_lin[:, P * tb:P * tb + P], src[:, tb, P * c:P * c + P], cst[:, 0, :])
                mm.then_inc(lin_full, 1)
            elif item in ("q0", "k0", "q1", "k1"):
                c, col = int(item[1]), C * (item[0] == "k")
                lin_unit(pe, turn, s, item)
                if (v := turn.at(lambda n: lin("xT1", n + 1))) is not None:
                    pe.wait_ge(lin_drained, v)
                products = [(w, x, k) for w, x in ((wqkv_hi, xT_hi), (wqkv_hi, xT_lo), (wqkv_lo, xT_hi)) for k in range(KC)]
                for j, (w, x, k) in enumerate(products):
                    mm = pe.matmul(ps_lin[:], w[:, k, col + P * c:col + P * c + P], x[:, k, :],
                                   start=(j == 0), stop=(j == len(products) - 1))
                mm.then_inc(lin_full, 1)
            elif item in ("v0", "v1"):
                u = int(item[1])
                lin_unit(pe, turn, s, item)
                if (v := turn.at(lambda n: lin("xT1", n + 1))) is not None:
                    pe.wait_ge(lin_drained, v)
                products = [(w, x, k) for w, x in ((wqkv_hi, xT_hi), (wqkv_hi, xT_lo), (wqkv_lo, xT_hi)) for k in range(KC)]
                for j in range(2):
                    tb = 2 * u + j
                    for m, (w, x, k) in enumerate(products):
                        mm = pe.matmul(ps_lin[:, C * j:C * j + C], x[:, k, P * tb:P * tb + P], w[:, k, 2 * C:3 * C],
                                       start=(m == 0), stop=(m == len(products) - 1))
                mm.then_inc(lin_full, 1)
            elif item in ("pj0", "pj1", "r0", "r1", "kv0", "kv1"):
                u, kind = int(item[-1]), item[:-1]
                x, w = {"pj": (y[(turn.parity + 1) % 2], wp), "r": (mix_r, wr), "kv": (kact, wv)}[kind]
                lin_unit(pe, turn, s, item)
                if kind == "pj":
                    if (v := turn.at(lambda n: KC * (n - 1 + 1))) is not None:
                        pe.wait_ge(y_norm, v)
                elif kind == "r":
                    if (v := turn.at(lambda n: 2 * KC * (n - 2 + 1))) is not None:
                        pe.wait_ge(mix_step, v)
                else:
                    if (v := turn.at(lambda n: KC * (n - 2 + 1))) is not None:
                        pe.wait_ge(sq_done, v)
                for j in range(2):
                    tb = 2 * u + j
                    for k in range(KC):
                        mm = pe.matmul(ps_lin[:, C * j:C * j + C], x[:, k, P * tb:P * tb + P], w[:, k, :],
                                       start=(k == 0), stop=(k == KC - 1))
                mm.then_inc(lin_full, 1)
            elif item in ("kk0", "kk1"):
                c = int(item[-1])
                lin_unit(pe, turn, s, item)
                if (v := turn.at(lambda n: 2 * KC * (n - 2 + 1))) is not None:
                    pe.wait_ge(mix_step, v)
                for k in range(KC):
                    mm = pe.matmul(ps_lin[:], wk[:, k, P * c:P * c + P], mix_k[:, k, :], start=(k == 0), stop=(k == KC - 1))
                mm.then_inc(lin_full, 1)

        @block.tensor
        def _(pe):
            pe.wait_ge(s_load, 16 * NLOADS)
            pe.wait_ge(s_setup, SETUP_ONES)
            for k in range(KC):
                pe.matmul(ps_lin[:, 0:C], bvcol[:, k:k + 1].to_broadcast([P, P]), wp[:, k, :], start=(k == 0), stop=False)
            pe.matmul(ps_lin[:, 0:C], ones_row[:], bprow[:], start=False, stop=True).then_inc(s_bias_mm, 1)
            pe.wait_ge(s_ready, 1)
            for turn in turns(pe):
                for s in range(NG):
                    for item in STEPS[s]:
                        if turn.has(item, s) if item in BATCH or item in GROUP else False:
                            tensor_part(pe, turn, s, item)

        def full(engine, turn, item):
            if (v := turn.at(lambda n: lin(item, n + LIN_BATCH[item]))) is not None:
                engine.wait_ge(lin_full, v)

        def scalar_part(act, turn, s, item):
            if item[0] == "U":
                k = int(item[1:])
                sbk, heads = EXP_TILES[k]
                slot = k % 2
                width = T - P * sbk
                if (v := turn.at(lambda n: NE * (NG * n + s - 2) + k + 1)) is not None:
                    act.wait_ge(exp_full, v)
                if (v := turn.at(lambda n: TB * (NG * n + s - 2 - 1) + sbk + 1)) is not None:
                    act.wait_ge(pv_done, v)
                dst = probs[sbk][:, heads[0]:heads[-1] + 1, :]
                if len(heads) == 2:
                    src = ps_exp[:, slot, :, 0:width]
                else:
                    flat = ps_exp[:, slot, :, :].rearrange("p a t -> p (a t)")[:, 0:HG * width]
                    src, dst = flat, dst.rearrange("p h t -> p (h t)")
                act.activation(dst, src, ACT.Exp, scale=SCALE).then_inc(exp_done, 1)
            elif item == "PV3":
                g = (s - 3) % NG
                if (v := turn.at(lambda n: TB * (NG * n + s - 3 + 1))) is not None:
                    act.wait_ge(pv_done, v)
                if (v := turn.at(lambda n: 32 * ((NG * n + s - 3 - 2) // NG + 1))) is not None:
                    act.wait_ge(y_in[(g - 2) % NG], v)
                act.activation(y_raw[:, g % 2, :], ps_pv[:], ACT.Copy).then_inc(y_out, 1)
            elif item == "mT":
                g = (s - 1) % NG
                if (v := turn.at(lambda n: lin("mT", NG * n + s - 1))) is not None:
                    act.wait_ge(lin_full, v)
                if (v := turn.at(lambda n: 32 * ((NG * n + s - 1 - 2) // NG + 1))) is not None:
                    act.wait_ge(max_in[(g - 2) % NG], v)
                act.activation(maxT[:, g % 2, 0, :], ps_lin[0:HG * TB, 0:P], ACT.Copy).then_inc(max_hi, 1)
            elif item[:2] == "eT":
                c = int(item[2])
                rows = P if c < EC - 1 else EL
                full(act, turn, item)
                if (v := turn.at(lambda n: lin("h1", n))) is not None:
                    act.wait_ge(lin_full, v)
                act.activation(embT[0:rows, c, :], ps_lin[0:rows, :], ACT.Copy).then_inc(lin_drained, 1)
            elif item[:2] == "xT":
                c = int(item[2])
                full(act, turn, item)
                if (v := turn.at(lambda n: max(lin("k1", n), lin("v1", n)))) is not None:
                    act.wait_ge(lin_full, v)
                act.activation(xT_hi[:, c, :], ps_lin[:], ACT.Copy).then_inc(xT_hi_done, 1)
            elif item in ("q0", "k0", "q1", "k1"):
                c, j = int(item[1]), int(item[0] == "k")
                full(act, turn, item)
                if (v := turn.at(lambda n: KC * (n + 1) + c)) is not None:
                    act.wait_ge(split_lo, v)
                act.activation(raw[:, j, :], ps_lin[:], ACT.Identity, bias=bqk[:, 2 * j + c:2 * j + c + 1]).then_inc(lin_drained, 1)
            elif item in ("v0", "v1"):
                u = int(item[1])
                par = (turn.parity + 1) % 2
                full(act, turn, item)
                if (v := turn.at(lambda n: TB * NG * (n + 1 - 2 + 1))) is not None:
                    act.wait_ge(pv_done, v)
                act.activation(vx[par][:, 2 * u:2 * u + 2, :, 0], ps_lin[:].rearrange("p (t c) -> p t c", t=2),
                               ACT.Copy).then_inc(lin_drained, 1)
            elif item in ("hi0", "hi1"):
                c = int(item[2])
                if (v := turn.at(lambda n: 3 * (KC * (n + 1) + c + 1))) is not None:
                    act.wait_ge(rope_step, v)
                for g in (2 * c, 2 * c + 1):
                    if (v := turn.at(lambda n: 16 * NSTACK * (n + 1))) is not None:
                        act.wait_ge(stack_in[g], v)
                act.activation(parts[0][:, c, :, :], raw[:], ACT.Copy).then_inc(split_hi, 1)
            elif item in ("mi0", "mi1"):
                c = int(item[2])
                if (v := turn.at(lambda n: KC * (n + 1) + c + 1)) is not None:
                    act.wait_ge(split_rest, v)
                act.activation(parts[1][:, c, :, :], raw[:], ACT.Copy).then_inc(split_mid, 1)
            elif item in ("x2T0", "x2T1"):
                c = int(item[3])
                full(act, turn, item)
                if (v := turn.at(lambda n: 2 * KC * (n - 2))) is not None:
                    act.wait_ge(mix_step, v)
                act.activation(x2T[:, c, 1:T + 1], ps_lin[:], ACT.Copy).then_inc(lin_drained, 1)
            elif item in ("kk0", "kk1"):
                c = int(item[2])
                full(act, turn, item)
                if (v := turn.at(lambda n: lin("kv1", n - 3))) is not None:
                    act.wait_ge(lin_full, v)
                act.activation(kact[:, c, :], ps_lin[:], ACT.Relu).then_inc(lin_drained, 1)
            elif item in ("r0", "r1"):
                u = int(item[1])
                full(act, turn, item)
                if (v := turn.at(lambda n: 16 * (n - 2))) is not None:
                    act.wait_ge(stored, v)
                act.activation(gate[:, 2 * u:2 * u + 2, :], ps_lin[:].rearrange("p (t c) -> p t c", t=2),
                               ACT.Tanh, scale=0.5).then_inc(lin_drained, 1)

        @block.scalar
        def _(act):
            act.wait_ge(s_load, 16 * NLOADS)
            act.wait_ge(s_ready, 1)
            for turn in turns(act):
                for s in range(NG):
                    for item in STEPS[s]:
                        if turn.has(item, s) if item in BATCH or item in GROUP else False:
                            scalar_part(act, turn, s, item)

        def ln_stats(dve, turn, j, x, off, last_unit):
            a = ln[j]
            if (v := turn.at(lambda n: lin(last_unit, n + off))) is not None:
                dve.wait_ge(lin_drained, v)
            for tb in range(TB):
                dve.bn_stats(a["stats"][:, tb, :], x[:, tb, :]).then_inc(ln_step[j], 1)
            if (v := turn.at(lambda n: 9 * (n + off) + TB)) is not None:
                dve.wait_ge(ln_step[j], v)
                dve.sem_inc(passed["dve"], 1)
            if (v := turn.at(lambda n: TB * (n + off))) is not None:
                dve.wait_ge(ln_out[j], v)
                dve.sem_inc(passed["dve"], 1)
            for tb in range(TB):
                dve.bn_aggr(a["mv"][:, tb, :], a["stats"][:, tb, :]).then_inc(ln_step[j], 1)
            if (v := turn.at(lambda n: 9 * (n + off) + 2 * TB)) is not None:
                dve.wait_ge(ln_step[j], v)
            dve.tensor_scalar(a["var"][:], a["mv"][:, :, 1], EPS, None, ALU.add).then_inc(ln_step[j], 1)

        def ln_normalise(dve, turn, j, x, to, off, reader):
            a = ln[j]
            if (v := turn.at(lambda n: n + off + 1)) is not None:
                dve.wait_ge(ln_rstd[j], v)
            if (v := turn.at(lambda n: lin(reader, n + off - 1))) is not None:
                dve.wait_ge(lin_full, v)
            for tb in range(TB):
                dve.tensor_scalar(to[:, tb, :], x[:, tb, :], a["mv"][:, tb, 0:1], a["rstd"][:, tb:tb + 1],
                                  ALU.subtract, ALU.mult).then_inc(ln_out[j], 1)

        def vector_part(dve, turn, s, item):
            if item[0] == "M":
                k = int(item[1:])
                tb, heads = MAX_TILES[k]
                slot = (s + k) % 2
                width = P * (tb + 1)
                if (v := turn.at(lambda n: NM * (NG * n + s) + k + 1)) is not None:
                    dve.wait_ge(max_full, v)
                src = ps_max[:, slot, 0:width * len(heads)].rearrange("p (h t) -> p h t", h=len(heads))
                dst = rowmax[:, s % 2, :].rearrange("p (h t) -> p h t", h=HG)[:, heads[0]:heads[-1] + 1, tb]
                dve.tensor_reduce(dst, src, AX.X, ALU.max).then_inc(max_done, 1)
            elif item == "mT":
                g = (s - 1) % NG
                if (v := turn.at(lambda n: NG * n + s - 1 + 1)) is not None:
                    dve.wait_ge(max_hi, v)
                dve.tensor_tensor(maxT[:, g % 2, 1, :], ps_lin[0:HG * TB, 0:P], maxT[:, g % 2, 0, :],
                                  ALU.subtract).then_inc(lin_drained, 1)
            elif item == "idx":
                if (v := turn.at(lambda n: 16 * (n + 2 + 1))) is not None:
                    dve.wait_ge(ids_in, v)
                dve.tensor_scalar(row_t[:], ids_sb[:], 1.0, 0.0, ALU.add, ALU.max).then_inc(rows_done, 1)
                if (v := turn.at(lambda n: 2 * (n + 2) + 1)) is not None:
                    dve.wait_ge(rows_done, v)
                if (v := turn.at(lambda n: 16 * TB * (n + 2))) is not None:
                    dve.wait_ge(gathered, v)
                dve.tensor_scalar(row_id[:], row_t[:], float(ROWS + 1), None, ALU.min).then_inc(rows_done, 1)
            elif item in ("h0", "h1"):
                u = int(item[1])
                full(dve, turn, item)
                if (v := turn.at(lambda n: n + 1)) is not None:
                    dve.wait_ge(hb_done, v)
                if (v := turn.at(lambda n: TB * (n + 1))) is not None:
                    dve.wait_ge(ln_out[0], v)
                dve.tensor_copy(h[:, 2 * u:2 * u + 2, :], ps_lin[:].rearrange("p (t c) -> p t c", t=2)).then_inc(lin_drained, 1)
            elif item == "ln1a":
                ln_stats(dve, turn, 0, h, 1, "h1")
            elif item == "ln1n":
                ln_normalise(dve, turn, 0, h, xn, 1, "xT1")
            elif item == "ln2a":
                ln_stats(dve, turn, 1, h1, -1, "pj1")
            elif item == "ln2n":
                ln_normalise(dve, turn, 1, h1, xn2, -1, "x2T1")
            elif item in ("xT0", "xT1"):
                c = int(item[2])
                if (v := turn.at(lambda n: KC * (n + 1) + c + 1)) is not None:
                    dve.wait_ge(xT_hi_done, v)
                dve.tensor_tensor(xT_lo[:, c, :], ps_lin[:], xT_hi[:, c, :].bitcast(F32), ALU.subtract).then_inc(lin_drained, 1)
            elif item in ("tt0", "tt1"):
                c = int(item[2])
                if (v := turn.at(lambda n: KC * (n + 1) + c + 1)) is not None:
                    dve.wait_ge(split_hi, v)
                dve.tensor_tensor(raw[:], raw[:], parts[0][:, c, :, :], ALU.subtract).then_inc(split_rest, 1)
            elif item in ("lo0", "lo1"):
                c = int(item[2])
                if (v := turn.at(lambda n: KC * (n + 1) + c + 1)) is not None:
                    dve.wait_ge(split_mid, v)
                dve.tensor_tensor(parts[2][:, c, :, :], raw[:], parts[1][:, c, :, :], ALU.subtract).then_inc(split_lo, 1)
            elif item == "rc":
                g = (s - 3) % NG
                if (v := turn.at(lambda n: 32 * ((NG * n + s - 3) // NG + 1))) is not None:
                    dve.wait_ge(y_in[g], v)
                if (v := turn.at(lambda n: 16 * ((NG * n + s - 3) // NG))) is not None:
                    dve.wait_ge(inv_out[g], v)
                dve.reciprocal(inv_sums[:, g, :], sums[:, g, :]).then_inc(inv_done, 1)
            elif item in ("yn0", "yn1"):
                c = int(item[2])
                for g in (2 * c, 2 * c + 1):
                    if (v := turn.at(lambda n: 32 * (n - 1 + 1))) is not None:
                        dve.wait_ge(y_in[g], v)
                    if (v := turn.at(lambda n: 16 * (n - 1 + 1))) is not None:
                        dve.wait_ge(inv_in[g], v)
                yb = y[(turn.parity + 1) % 2][:, c, :]
                dve.tensor_tensor(yb, yb, inv_rows[:, c, :], ALU.mult).then_inc(y_norm, 1)
            elif item in ("pj0", "pj1"):
                u = int(item[2])
                par = (turn.parity + 1) % 2
                full(dve, turn, item)
                if (v := turn.at(lambda n: n - 1 + 1)) is not None:
                    dve.wait_ge(hb_done, v)
                if (v := turn.at(lambda n: TB * (n - 1))) is not None:
                    dve.wait_ge(ln_out[1], v)
                if (v := turn.at(lambda n: n - 1)) is not None:
                    dve.wait_ge(fin_done, v)
                dve.tensor_tensor(h1[:, 2 * u:2 * u + 2, :], ps_lin[:].rearrange("p (t c) -> p t c", t=2),
                                  hb[par][:, 2 * u:2 * u + 2, :], ALU.add).then_inc(lin_drained, 1)
            elif item in ("mm0", "mm1"):
                c = int(item[2])
                before = x2T[:, c, 0:T]
                if (v := turn.at(lambda n: KC * (n - 2) + c + 1)) is not None:
                    dve.wait_ge(mix_diff, v)
                if (v := turn.at(lambda n: lin("r1", n - 3))) is not None:
                    dve.wait_ge(lin_full, v)
                dve.scalar_tensor_tensor(out=mix_r[:, c, :], in0=mix_k[:, c, :], scalar=muc[:, 0, c:c + 1], in1=before,
                                         op0=ALU.mult, op1=ALU.add).then_inc(mix_step, 1)
                if (v := turn.at(lambda n: 2 * (KC * (n - 2) + c) + 1)) is not None:
                    dve.wait_ge(mix_step, v)
                dve.scalar_tensor_tensor(out=mix_k[:, c, :], in0=mix_k[:, c, :], scalar=muc[:, 1, c:c + 1], in1=before,
                                         op0=ALU.mult, op1=ALU.add).then_inc(mix_step, 1)
            elif item in ("sq0", "sq1"):
                c = int(item[2])
                if (v := turn.at(lambda n: lin(f"kk{c}", n - 2))) is not None:
                    dve.wait_ge(lin_drained, v)
                dve.tensor_tensor(kact[:, c, :], kact[:, c, :], kact[:, c, :], ALU.mult).then_inc(sq_done, 1)
            elif item in ("kv0", "kv1"):
                u = int(item[2])
                full(dve, turn, item)
                if (v := turn.at(lambda n: lin("r1", n - 2))) is not None:
                    dve.wait_ge(lin_drained, v)
                half = gate[:, 2 * u:2 * u + 2, :]
                dve.scalar_tensor_tensor(out=half, in0=half, scalar=1.0, in1=ps_lin[:].rearrange("p (t c) -> p t c", t=2),
                                         op0=ALU.add, op1=ALU.mult).then_inc(lin_drained, 1)
            elif item == "fin":
                if (v := turn.at(lambda n: lin("kv1", n - 2))) is not None:
                    dve.wait_ge(lin_drained, v)
                dve.scalar_tensor_tensor(out=gate[:], in0=gate[:], scalar=0.5, in1=h1[:], op0=ALU.mult,
                                         op1=ALU.add).then_inc(fin_done, 1)

        @block.vector
        def _(dve):
            dve.memset(ones_row[:], 1.0).then_inc(s_setup, 1)
            dve.memset(minus_half[:], -0.5)
            for v in vx:
                dve.memset(v[:, :, :, 1], 1.0)
            dve.memset(x2T[:, :, 0:1], 0.0)
            dve.memset(ks[KS:KM, :, :], -1.0)
            dve.wait_ge(s_load, 16 * NLOADS)
            dve.tensor_copy(ident_bf[:], cst[:, 0, :])
            dve.tensor_copy(mask_bf[:], cst[:, 1, :])
            dve.tensor_copy(wqkv_hi[:], stage).then_inc(s_setup, 1)
            dve.wait_ge(s_setup, 2)
            dve.tensor_tensor(wqkv_lo[:], stage, wqkv_hi[:].bitcast(F32), ALU.subtract)
            dve.wait_ge(s_bias_mm, 1)
            dve.tensor_copy(bias_p[:], ps_lin[:, 0:C]).then_inc(s_ready, 1)
            for turn in turns(dve):
                for s in range(NG):
                    for item in STEPS[s]:
                        if turn.has(item, s) if item in BATCH or item in GROUP else False:
                            vector_part(dve, turn, s, item)

        def gpsimd_part(pool, turn, s, item):
            if item[0] == "U":
                k = int(item[1:])
                if k + 1 not in EXP_TILES_UPTO:
                    return
                sbk = EXP_TILES_UPTO.index(k + 1)
                if (v := turn.at(lambda n: NE * (NG * n + s - 2) + k + 1)) is not None:
                    pool.wait_ge(exp_done, v)
                    pool.sem_inc(passed["pool"], 1)
                diag = probs[sbk][:, :, 0:P]
                pool.affine_select(out=diag, in_=diag, compare_op=ALU.is_ge, fill=0.0, base=0,
                                   pattern=[[0, HG], [1, P]], channel_multiplier=-1).then_inc(masked, 1)
            elif item == "gather":
                if (v := turn.at(lambda n: 2 * (n + 2 + 1))) is not None:
                    pool.wait_ge(rows_done, v)
                if (v := turn.at(lambda n: lin("eT2", n + 1))) is not None:
                    pool.wait_ge(lin_full, v)
                    pool.sem_inc(passed["pool"], 1)
                for tb in range(TB):
                    pool.indirect_dma_start(out=emb[:, tb, :], out_offset=None, in_=table,
                                            in_offset=bass.IndirectOffsetOnAxis(ap=row_id[:, tb:tb + 1], axis=0)
                                            ).then_inc(gathered, 16)
            elif item in ("ln1p", "ln2p"):
                j = int(item[2]) - 1
                off = BATCH[item]
                if (v := turn.at(lambda n: 9 * (n + off + 1))) is not None:
                    pool.wait_ge(ln_step[j], v)
                if (v := turn.at(lambda n: TB * (n + off))) is not None:
                    pool.wait_ge(ln_out[j], v)
                pool.tensor_tensor(ln[j]["rstd"][:], ln[j]["var"][:], minus_half[:], ALU.pow).then_inc(ln_rstd[j], 1)
            elif item in ("rp0", "rp1"):
                c = int(item[2])
                cs = [rope[:, j, :].unsqueeze(1).to_broadcast([P, 2, T]) for j in range(2)]
                if (v := turn.at(lambda n: 64 * (n + 1 + 1))) is not None:
                    pool.wait_ge(swap_in[c], v)
                pool.tensor_tensor(raw[:], raw[:], cs[0], ALU.mult).then_inc(rope_step, 1)
                pool.tensor_tensor(swapped[:], swapped[:], cs[1], ALU.mult).then_inc(rope_step, 1)
                if (v := turn.at(lambda n: 3 * (KC * (n + 1) + c) + 2)) is not None:
                    pool.wait_ge(rope_step, v)
                pool.tensor_tensor(raw[:], raw[:], swapped[:], ALU.add).then_inc(rope_step, 1)
            elif item in ("mix0", "mix1"):
                c = int(item[3])
                x, before = x2T[:, c, 1:T + 1], x2T[:, c, 0:T]
                if (v := turn.at(lambda n: lin(f"x2T{c}", n - 2))) is not None:
                    pool.wait_ge(lin_drained, v)
                if (v := turn.at(lambda n: lin("kk1", n - 3))) is not None:
                    pool.wait_ge(lin_full, v)
                pool.tensor_tensor(mix_k[:, c, :], x, before, ALU.subtract).then_inc(mix_diff, 1)
            elif item == "hb":
                par = (turn.parity + 1) % 2
                if (v := turn.at(lambda n: lin("h1", n + 1))) is not None:
                    pool.wait_ge(lin_drained, v)
                if (v := turn.at(lambda n: lin("pj1", n - 1))) is not None:
                    pool.wait_ge(lin_drained, v)
                pool.tensor_tensor(hb[par][:], h[:], bias_p[:].unsqueeze(1).to_broadcast([P, TB, C]),
                                   ALU.add).then_inc(hb_done, 1)


        @block.gpsimd
        def _(pool):
            pool.wait_ge(s_load, 16 * NLOADS)
            pool.wait_ge(s_ready, 1)
            for turn in turns(pool):
                for s in range(NG):
                    for item in STEPS[s]:
                        if turn.has(item, s) if item in BATCH or item in GROUP else False:
                            gpsimd_part(pool, turn, s, item)

NLOADS = 13
SETUP_ONES = 1


def kernel(**inputs):
    import concourse.bacc as bacc
    from concourse.bass_utils import run_bass_kernel_spmd

    def arr(name):
        return np.ascontiguousarray(inputs[name])

    f = np.float32
    ids = np.ascontiguousarray(arr("x").reshape(B, TB, P).transpose(0, 2, 1))
    t0, t1, t2 = arr("L0_tok_t0"), arr("L0_tok_t1"), arr("L0_tok_t2")
    table = np.zeros((ROWS + 2, EW), f)
    r1, r2 = 1 + len(t0), 1 + len(t0) + len(t1)
    table[1:r1, 0:E0] = t0
    table[r1:r2, E0:E0 + E1] = t1
    table[r2:r2 + len(t2), E0 + E1:EW] = t2
    w_tok = np.concatenate([arr("L0_tok_w0"), arr("L0_tok_w1"), arr("L0_tok_w2")], axis=0)
    order = np.arange(C).reshape(KC, 2, HG, D).transpose(0, 1, 3, 2).reshape(-1)
    w_qkv = np.concatenate([arr("L0_attn_wq").T[:, order], arr("L0_attn_wk").T[:, order], arr("L0_attn_wv").T], axis=1)
    b_qk = np.concatenate([arr("L0_attn_bq")[order].reshape(KC, P), arr("L0_attn_bk")[order].reshape(KC, P)]).T
    b_v = arr("L0_attn_bv").reshape(KC, P).T
    mu = np.stack([arr("L0_ffn_mu_r").reshape(KC, P).T, arr("L0_ffn_mu_k").reshape(KC, P).T], axis=1)
    half = D // 2
    i = np.arange(half, dtype=f)
    alpha = (f(1.0) / np.power(f(10000.0), f(2.0) * i / f(D))).astype(f)
    ang = (np.arange(T, dtype=f)[:, None] * alpha).astype(f)
    d_of = (np.arange(P) // HG) % D
    cos = np.cos(ang).astype(f).T[d_of % half]
    sin = np.sin(ang).astype(f).T[d_of % half] * np.where(d_of < half, f(-1), f(1))[:, None]
    cos_sin = np.stack([cos, sin], axis=1).astype(f)
    consts = np.stack([np.eye(P, dtype=f), np.triu(np.full((P, P), MASKED, f), 1)], axis=1)
    arrays = dict(ids=ids, table=table, w_tok=w_tok, w_qkv=w_qkv, b_qk=b_qk, w_p=arr("L0_attn_wp").T, b_v=b_v,
                  b_p=arr("L0_attn_bp").reshape(1, C), w_r=arr("L0_ffn_W_r").T, w_k=arr("L0_ffn_W_k").T,
                  w_v=arr("L0_ffn_W_v").T, mu=mu, cos_sin=cos_sin, consts=consts)
    arrays = {name: np.ascontiguousarray(a) for name, a in arrays.items()}

    nc = bacc.Bacc("TRN2", target_bir_lowering=False, num_devices=1)
    args = {name: nc.dram_tensor(f"in_{name}", a.shape, mybir.dt.from_np(a.dtype), kind="ExternalInput").ap()
            for name, a in arrays.items()}
    out = nc.dram_tensor("out_h", (B, T, C), F32, kind="ExternalOutput").ap()
    tower(nc, out=out.rearrange("b (k p) c -> b p k c", p=P), **args)
    r = run_bass_kernel_spmd(nc, [{f"in_{name}": a for name, a in arrays.items()}], core_ids=[0])
    return r.results[0]["out_h"]
```

```python
from contextlib import ExitStack

import concourse.bass as bass
import numpy as np
from concourse import mybir

ALU = mybir.AluOpType
ACT = mybir.ActivationFunctionType
AX = mybir.AxisListType
F32, F32R, BF16, I32, U32 = (mybir.dt.float32, mybir.dt.float32r, mybir.dt.bfloat16, mybir.dt.int32,
                             mybir.dt.uint32)

P = 128
B, T, C, H = 32, 512, 256, 16
D = C // H
TB = T // P
KC = C // P
HG = 4
NG = H // HG
E0, E1, E2 = 256, 64, 16
EW = E0 + E1 + E2
EC = (EW + P - 1) // P
EL = EW - (EC - 1) * P
ROWS = 25000
NPART = 3
NCOMB = 6
Q_PART = (0, 1, 2, 0, 1, 0)
K_PART = (0, 0, 0, 1, 1, 2)
KS = NCOMB * D
KM = KS + 2
SCALE = float(D) ** -0.5
EPS = 1e-5
MASKED = -1e30

MAX_TILES = ([(3, (h,)) for h in range(HG)] + [(2, (h,)) for h in range(HG)]
             + [(1, (0, 1)), (1, (2, 3)), (0, (0, 1, 2, 3))])
NM = len(MAX_TILES)
EXP_TILES = ([(0, (h,)) for h in range(HG)] + [(1, (h,)) for h in range(HG)]
             + [(2, (0, 1)), (2, (2, 3)), (3, (0, 1, 2, 3))])
NE = len(EXP_TILES)
EXP_BANKS = 3
EXP_TILES_UPTO = tuple(max(k for k, (sb, _) in enumerate(EXP_TILES) if sb == b) + 1 for b in range(TB))

STEPS = [" ".join(lines).split() for lines in (
    [
        "eT0 eT1 U0 M0 U1 M1 eT2 st10 U2 st11 PV2 M2 U3 PV3 xload st12 M3 x2T0 mT mix0 U4 mix1 U5 rb M4 M5",
        "x2T1 idx M6 ln1a0 U6 M7 U7 U8 PV0 h0 rc U9 st20 M8 ln1a1 h1 U10 ln1p ln1v M9 M10 PV1 gather ln1n0",
    ],
    [
        "U0 U1 PV2 M0 ln1n1 PV3 mT M1 U2 U3 st21 U4 M2 xT0 xT1 mm0 mm1 M3 U5 M4 U6 PV0 q0 U7 k0 kk0 rc M5 U8",
        "sq0 kk1 st22 rcos00 sw0 M6 M7 PV1 M8 M9 rb U9 rcos01 U10 M10",
    ],
    [
        "U0 M0 U1 U2 M1 st30 rsin00 mT v0 PV2 rsin01 M2 PV3 st31 M3 yn0 U3 M4 U4 r0 tt00 sq1 M5 v1 tt01",
        "radd00 hi00 U5 hi01 M6 st32 rc PV0 sw1 lo00 U6 md00 md01 radd01 lo01 U7 q1 M7 k1 U8 M8 U9 U10 rb M9",
        "r1 rcos10 rsin10 M10 PV1",
    ],
    [
        "U0 M0 radd10 mT kv0 M1 M2 st00 yn1 rcos11 PV2 PV3 rsin11 M3 U1 fin0 U2 M4 kv1 U3 out hi10 M5 U4 md10",
        "hi11 fin1 U5 tt10 radd11 pj0 M6 tt11 hb0 pj1 ln2a0 ln2a1 PV0 U6 M7 rc U7 ln2v st01 st02 M8 lo10 U8",
        "md11 U9 M9 ln2p ln2n0 PV1 M10 U10 hb1 ln2n1 rb lo11",
    ],
)]
LIN_BATCH = {"eT0": 1, "eT1": 1, "eT2": 1, "h0": 1, "h1": 1, "xT0": 1, "xT1": 1, "q0": 1, "k0": 1,
             "q1": 1, "k1": 1, "v0": 1, "v1": 1, "pj0": -1, "pj1": -1, "x2T0": -2, "x2T1": -2,
             "kk0": -2, "kk1": -2, "r0": -2, "r1": -2, "kv0": -2, "kv1": -2}
BATCH = dict(LIN_BATCH, xload=2, idx=2, gather=2, ln1a0=1, ln1a1=1, ln1v=1, ln1p=1, ln1n0=1, ln1n1=1, sw0=1, sw1=1,
             hb0=1, hb1=1, yn0=-1, yn1=-1, ln2a0=-1, ln2a1=-1, ln2v=-1, ln2p=-1,
             ln2n0=-1, ln2n1=-1, mix0=-2, mix1=-2, mm0=-2, mm1=-2, sq0=-2, sq1=-2, fin0=-2, fin1=-2, out=-2)
BATCH.update({f"st{g}{third}": 1 if g == 0 else 0 for g in range(NG) for third in range(3)})
BATCH.update({f"{step}{c}{j}": 1 for step in ("rcos", "rsin", "radd", "hi", "tt", "md", "lo") for c in range(KC) for j in range(2)})
GROUP = {"mT": -1, "rc": -3, "rb": -3, "PV0": -2, "PV1": -2, "PV2": -3, "PV3": -3}
GROUP.update({f"U{k}": -2 for k in range(NE)})
GROUP.update({f"M{k}": 0 for k in range(NM)})

FIRST_N, LAST_N = -2, B + 1
LOOP_FROM, LOOP_TO = 4, 30


def batch_ok(b):
    return 0 <= b < B


def lin_units(n):
    position = 0
    for s in range(NG):
        for item in STEPS[s]:
            if item in LIN_BATCH or item == "mT":
                key = n + LIN_BATCH[item] if item in LIN_BATCH else NG * n + s - 1
                if 0 <= key < (B if item in LIN_BATCH else NG * B):
                    yield item, key, position % 2
                position += 1


def count_lin_units():
    seen, in_bank, n_units, n_bank = {}, {}, 0, [0, 0]
    for n in range(FIRST_N, LAST_N + 1):
        for item, key, bank in lin_units(n):
            n_units += 1
            n_bank[bank] += 1
            seen[item, key], in_bank[item, key] = n_units, n_bank[bank]
    return seen, in_bank


LIN, LIN_IN_BANK = count_lin_units()
LIN_BANK = {item if item != "mT" else (item, (key + 1) % NG): bank for item, key, bank in lin_units(4)}


class Turn:

    def __init__(self, n=None, register=None, offset=0):
        self.register, self.offset = register, offset
        self.ns = [n] if register is None else list(range(LOOP_FROM + offset, LOOP_TO + offset, 2))
        self.parity = self.ns[0] % 2

    def has(self, item, s):
        def ok(n):
            if item in GROUP:
                return 0 <= NG * n + s + GROUP[item] < NG * B
            return batch_ok(n + BATCH[item])
        return all(ok(n) for n in self.ns)

    def at(self, count):
        if all(count(n) <= 0 for n in self.ns):
            return None
        return self.value(count)

    def value(self, count):
        vs = [count(n) for n in self.ns]
        if self.register is None:
            return vs[0]
        slope = (vs[-1] - vs[0]) // (self.ns[-1] - self.ns[0])
        assert all(v == vs[0] + slope * (n - self.ns[0]) for v, n in zip(vs, self.ns)) and vs[0] > 0
        return self.register * slope + (vs[0] - slope * (self.ns[0] - self.offset))


def turns(engine):
    for n in range(FIRST_N, LOOP_FROM):
        yield Turn(n)
    with engine.Fori(LOOP_FROM, LOOP_TO - 1, 2) as register:
        for offset in range(2):
            yield Turn(register=register, offset=offset)
    for n in range(LOOP_TO, LAST_N + 1):
        yield Turn(n)


def bank_of(s, item):
    return LIN_BANK.get((item, s) if item == "mT" else item)


def lin(unit, key):
    return LIN.get((unit, key), 0)


def out_of(unit, key):
    return LIN_IN_BANK.get((unit, key), 0)


def tower(nc, ids, table, w_tok, w_qkv, b_qk, w_p, b_v, b_p, w_r, w_k, w_v, mu, cos_sin, consts, out):
    with ExitStack() as ctx:
        def sb(name, shape, dt=F32):
            return ctx.enter_context(nc.sbuf_tensor(name, shape, dt))

        def psum(name, shape):
            return ctx.enter_context(nc.psum_tensor(name, shape, F32))

        def sem(name):
            return ctx.enter_context(nc.semaphore(name))

        ps_exp = psum("ps_exp", [P, EXP_BANKS, T])
        ps_max = psum("ps_max", [P, 2, T])
        ps_pv = psum("ps_pv", [P, T])
        ps_lin = [psum(f"ps_lin{j}", [P, T]) for j in range(2)]

        wtok = sb("wtok", [P, EC, C])
        wqkv_hi = sb("wqkv_hi", [P, KC, 3 * C], F32R)
        wqkv_lo = sb("wqkv_lo", [P, KC, 3 * C], F32R)
        wp = sb("wp", [P, KC, C])
        wr = sb("wr", [P, KC, C])
        wk = sb("wk", [P, KC, C])
        wv = sb("wv", [P, KC, C])
        bqk = sb("bqk", [P, 4])
        bvcol = sb("bvcol", [P, KC])
        bprow = sb("bprow", [1, C])
        ones_row = sb("ones_row", [1, P])
        bias_p = sb("bias_p", [P, C])
        muc = sb("muc", [P, 2, KC])
        rope = sb("rope", [P, 2, T])
        cst = sb("cst", [P, 2, P])
        ident_bf = sb("ident_bf", [P, P], BF16)
        mask_bf = sb("mask_bf", [P, P], BF16)
        minus_half = sb("minus_half", [P, TB])
        ids_sb = sb("ids_sb", [P, TB], I32)
        row_t = sb("row_t", [P, TB], I32)
        row_id = sb("row_id", [P, TB], U32)
        emb = sb("emb", [P, TB, EW])
        embT = sb("embT", [P, EC, T])
        h = sb("h", [P, TB, C])
        xn = sb("xn", [P, TB, C])
        xT_hi = sb("xT_hi", [P, KC, T], F32R)
        xT_lo = sb("xT_lo", [P, KC, T], F32R)
        raw = sb("raw", [P, 2, T])
        swapped = sb("swapped", [P, 2, T])
        parts = [sb(f"part{j}", [P, KC, 2, T], BF16) for j in range(NPART)]
        qs = sb("qs", [KM, H, T], BF16)
        ks = sb("ks", [KM, H, T], BF16)
        vx = [sb(f"vx{p}", [P, TB, C, 2]) for p in range(2)]
        probs = [sb(f"probs{j}", [P, HG, T - P * j]) for j in range(TB)]
        rowmax = sb("rowmax", [P, 2, HG * TB])
        maxT = sb("maxT", [HG * TB, 2, 2, P], BF16)
        y_raw = sb("y_raw", [P, 2, T])
        y = [sb(f"y{p}", [P, KC, T]) for p in range(2)]
        sums = sb("sums", [P, NG, HG * T // P])
        inv_sums = sb("inv_sums", [P, NG, HG * T // P])
        inv_rows = sb("inv_rows", [P, KC, T])
        hb = [sb(f"hb{p}", [P, TB, C]) for p in range(2)]
        h1 = sb("h1", [P, TB, C])
        xn2 = sb("xn2", [P, TB, C])
        x2T = sb("x2T", [P, KC, T + 1])
        mix_r = sb("mix_r", [P, KC, T])
        mix_k = sb("mix_k", [P, KC, T])
        kact = sb("kact", [P, KC, T])
        gate = sb("gate", [P, TB, C])
        ln = [dict(stats=sb(f"ln_stats{j}", [P, TB, 6]), mv=sb(f"ln_mv{j}", [P, TB, 2]),
                   var=sb(f"ln_var{j}", [P, TB]), rstd=sb(f"ln_rstd{j}", [P, TB])) for j in range(2)]
        inv_dram = nc.dram_tensor("inv_dram", [NG, HG, T], F32, kind="Internal").ap()

        s_load = sem("s_load")
        s_setup = sem("s_setup")
        s_bias_mm = sem("s_bias_mm")
        s_ready = sem("s_ready")
        lin_full = sem("lin_full")
        lin_drained = [sem(f"lin_drained{j}") for j in range(2)]
        ids_in = sem("ids_in")
        rows_done = sem("rows_done")
        gathered = sem("gathered")
        ln_step = [sem(f"ln{j}_step") for j in range(2)]
        ln_rstd = [sem(f"ln{j}_rstd") for j in range(2)]
        ln_out = [sem(f"ln{j}_out") for j in range(2)]
        xT_hi_done = sem("xT_hi_done")
        swap_in = [sem(f"swap_in{c}") for c in range(KC)]
        rope_cos = sem("rope_cos")
        rope_sin = sem("rope_sin")
        rope_sum = sem("rope_sum")
        split_hi = sem("split_hi")
        split_rest = sem("split_rest")
        split_mid = sem("split_mid")
        split_lo = sem("split_lo")
        stack_in = [sem(f"stack_in{g}") for g in range(NG)]
        max_full = sem("max_full")
        max_done = sem("max_done")
        max_hi = sem("max_hi")
        max_in = [sem(f"max_in{g}") for g in range(NG)]
        exp_full = sem("exp_full")
        exp_done = sem("exp_done")
        masked = sem("masked")
        pv_done = sem("pv_done")
        y_out = sem("y_out")
        y_in = [sem(f"y_in{g}") for g in range(NG)]
        inv_done = sem("inv_done")
        inv_out = [sem(f"inv_out{g}") for g in range(NG)]
        inv_in = [sem(f"inv_in{g}") for g in range(NG)]
        y_norm = sem("y_norm")
        hb_done = sem("hb_done")
        mix_diff = sem("mix_diff")
        mix_step = sem("mix_step")
        sq_done = sem("sq_done")
        fin_done = sem("fin_done")
        stored = sem("stored")

        passed = {e: sem(f"passed_{e}") for e in ("sp", "dve", "pool")}
        NSTACK = 2 * NCOMB
        stage = probs[0].rearrange("p a b -> p (a b)")[:, 0:KC * 3 * C].rearrange("p (k c) -> p k c", k=KC)
        block = ctx.enter_context(nc.Block())

        def sync_part(sp, turn, s, item):
            if item == "xload" and turn.has(item, s):
                if (v := turn.at(lambda n: 2 * (n + 2))) is not None:
                    sp.wait_ge(rows_done, v)
                    sp.sem_inc(passed["sp"], 1)
                b = turn.value(lambda n: n + 2) if turn.register is not None else turn.ns[0] + 2
                src = ids[b] if isinstance(b, int) else ids[bass.ds(b, 1)].rearrange("a p t -> (a p) t")
                sp.dma_start(ids_sb[:], src).then_inc(ids_in, 16)
            elif item in ("sw0", "sw1") and turn.has(item, s):
                c = int(item[-1])
                if (v := turn.at(lambda n: out_of(f"k{c}", n + 1))) is not None:
                    sp.wait_ge(lin_drained[LIN_BANK[f"k{c}"]], v)
                    sp.sem_inc(passed["sp"], 1)
                for blk in range(4):
                    to, of = 32 * blk, 32 * (blk ^ 1)
                    sp.dma_start(swapped[to:to + 32, :, :], raw[of:of + 32, :, :]).then_inc(swap_in[c], 16)
            elif item[:2] == "st" and turn.has(item, s):
                g, third = int(item[2]), int(item[3])
                c, off = g // 2, BATCH[item]
                if (v := turn.at(lambda n: 2 * (KC * (n + off) + c + 1))) is not None:
                    sp.wait_ge(split_lo, v)
                    sp.sem_inc(passed["sp"], 1)
                if (v := turn.at(lambda n: NM * (NG * (n + off - 1) + g + 1))) is not None:
                    sp.wait_ge(max_full, v)
                    sp.sem_inc(passed["sp"], 1)
                if (v := turn.at(lambda n: NE * (NG * (n + off - 1) + g + 1))) is not None:
                    sp.wait_ge(exp_full, v)
                    sp.sem_inc(passed["sp"], 1)
                rows = slice(64 * (g % 2), 64 * (g % 2) + 64)
                for k in (2 * third, 2 * third + 1):
                    for j, (stack, part) in enumerate(((qs, Q_PART[k]), (ks, K_PART[k]))):
                        sp.dma_start(stack[D * k:D * k + D, HG * g:HG * g + HG, :],
                                     parts[part][rows, c, j, :]).then_inc(stack_in[g], 16)
            elif item == "mT" and turn.has(item, s):
                g = (s - 1) % NG
                if (v := turn.at(lambda n: out_of("mT", NG * n + s - 1))) is not None:
                    sp.wait_ge(lin_drained[LIN_BANK["mT", s]], v)
                    sp.sem_inc(passed["sp"], 1)
                for j in range(2):
                    sp.dma_start(qs[KS + j:KS + j + 1, HG * g:HG * g + HG, :], maxT[:, g % 2, j, :]).then_inc(max_in[g], 16)
            elif item == "PV3" and turn.has(item, s):
                g = (s - 3) % NG
                c = g // 2
                if (v := turn.at(lambda n: NG * n + s - 3 + 1)) is not None:
                    sp.wait_ge(y_out, v)
                    sp.sem_inc(passed["sp"], 1)
                if (v := turn.at(lambda n: lin("pj1", (NG * n + s - 3) // NG - 2))) is not None:
                    sp.wait_ge(lin_full, v)
                    sp.sem_inc(passed["sp"], 1)
                par = (turn.parity + (s - 3) // NG) % 2
                sp.dma_start(y[par][64 * (g % 2):64 * (g % 2) + 64, c, :], y_raw[0:P:2, g % 2, :]).then_inc(y_in[g], 16)
                sp.dma_start(sums[:, g, :], y_raw[1:P:32, g % 2, :]).then_inc(y_in[g], 16)
            elif item == "rb" and turn.has(item, s):
                g = (s - 3) % NG
                c = g // 2
                if (v := turn.at(lambda n: NG * n + s - 3 + 1)) is not None:
                    sp.wait_ge(inv_done, v)
                    sp.sem_inc(passed["sp"], 1)
                sp.dma_start(inv_dram[g].rearrange("h (q t) -> (h q) t", t=HG * T // P), inv_sums[:, g, :]).then_inc(inv_out[g], 16)
                if (v := turn.at(lambda n: 16 * ((NG * n + s - 3) // NG + 1))) is not None:
                    sp.wait_ge(inv_out[g], v)
                    sp.sem_inc(passed["sp"], 1)
                if (v := turn.at(lambda n: KC * ((NG * n + s - 3) // NG - 1) + c + 1)) is not None:
                    sp.wait_ge(y_norm, v)
                    sp.sem_inc(passed["sp"], 1)
                sp.dma_start(inv_rows[64 * (g % 2):64 * (g % 2) + 64, c, :],
                             inv_dram[g].unsqueeze(1).to_broadcast([HG, D, T])).then_inc(inv_in[g], 16)
            elif item == "out" and turn.has(item, s):
                if (v := turn.at(lambda n: 2 * (n - 2 + 1))) is not None:
                    sp.wait_ge(fin_done, v)
                    sp.sem_inc(passed["sp"], 1)
                b = turn.value(lambda n: n - 2) if turn.register is not None else turn.ns[0] - 2
                dst = out[b] if isinstance(b, int) else out[bass.ds(b, 1)].rearrange("a p k c -> (a p) k c")
                sp.dma_start(dst, gate[:]).then_inc(stored, 16)

        @block.sync
        def _(sp):
            loads = [(wtok[:, 0:EC - 1, :], w_tok[0:(EC - 1) * P, :].rearrange("(k p) c -> p k c", p=P)),
                     (wtok[0:EL, EC - 1, :], w_tok[(EC - 1) * P:EW, :]),
                     (stage, w_qkv.rearrange("(k p) c -> p k c", p=P))]
            loads += [(to, of.rearrange("(k p) c -> p k c", p=P)) for to, of in ((wp, w_p), (wr, w_r), (wk, w_k), (wv, w_v))]
            loads += [(bqk[:], b_qk), (bvcol[:], b_v), (bprow[:], b_p), (muc[:], mu), (rope[:], cos_sin), (cst[:], consts)]
            assert len(loads) == NLOADS
            for to, of in loads:
                sp.dma_start(to[:] if not isinstance(to, bass.AP) else to, of).then_inc(s_load, 16)
            sp.wait_ge(s_load, 16 * NLOADS)
            for turn in turns(sp):
                for s in range(NG):
                    for item in STEPS[s]:
                        sync_part(sp, turn, s, item)
            sp.wait_ge(stored, 16 * B)

        def lin_unit(pe, turn, s, item):
            key = (lambda n: NG * n + s - 1) if item == "mT" else (lambda n: n + LIN_BATCH[item])
            if (v := turn.at(lambda n: out_of(item, key(n)) - 1)) is not None:
                pe.wait_ge(lin_drained[bank_of(s, item)], v)

        def tensor_part(pe, turn, s, item):
            bank = bank_of(s, item)
            if item[0] == "M":
                k = int(item[1:])
                tb, heads = MAX_TILES[k]
                g = s
                slot = (g + k) % 2
                if k == 0:
                    if (v := turn.at(lambda n: 16 * NSTACK * (n + 1))) is not None:
                        pe.wait_ge(stack_in[g], v)
                if (v := turn.at(lambda n: NM * (NG * n + s) + k - 1)) is not None:
                    pe.wait_ge(max_done, v)
                width = P * (tb + 1)
                tile = ps_max[:, slot, 0:width * len(heads)].rearrange("p (h t) -> p h t", h=len(heads))
                pe.matmul(tile[:, :, P * tb:], ident_bf[:], mask_bf[:].unsqueeze(1).to_broadcast([P, len(heads), P]),
                          start=True, stop=False, skip_group_check=True)
                for j, hd in enumerate(heads):
                    hh = HG * g + hd
                    mm = pe.matmul(tile[:, j, :], qs[0:KS, hh, P * tb:P * tb + P], ks[0:KS, hh, 0:width],
                                   start=False, stop=(j == len(heads) - 1), skip_group_check=True)
                mm.then_inc(max_full, 1)
            elif item[0] == "U":
                k = int(item[1:])
                sbk, heads = EXP_TILES[k]
                g = (s - 2) % NG
                slot = k % EXP_BANKS
                if k == 0:
                    if (v := turn.at(lambda n: 32 * ((NG * n + s - 2) // NG + 1))) is not None:
                        pe.wait_ge(max_in[g], v)
                back = EXP_BANKS if k >= EXP_BANKS else NE - max(m for m in range(NE) if m % EXP_BANKS == slot) + k
                if (v := turn.at(lambda n: NE * (NG * n + s - 2) + k - back + 1)) is not None:
                    pe.wait_ge(exp_done, v)
                width = T - P * sbk
                for j, hd in enumerate(heads):
                    hh = HG * g + hd
                    mm = pe.matmul(ps_exp[:, slot, width * j:width * j + width], ks[:, hh, P * sbk:P * sbk + P],
                                   qs[:, hh, P * sbk:T], start=(j == 0), stop=(j == len(heads) - 1),
                                   skip_group_check=True)
                mm.then_inc(exp_full, 1)
            elif item[0:2] == "PV":
                sbk = int(item[2])
                g = (s + GROUP[item]) % NG
                off = GROUP[item]
                par = (turn.parity + (s + off) // NG) % 2
                if (v := turn.at(lambda n: TB * (NG * n + s + off) + sbk + 1)) is not None:
                    pe.wait_ge(masked, v)
                if sbk == 0:
                    if (v := turn.at(lambda n: NG * n + s + off)) is not None:
                        pe.wait_ge(y_out, v)
                    if (v := turn.at(lambda n: out_of("v1", (NG * n + s + off) // NG))) is not None:
                        pe.wait_ge(lin_drained[LIN_BANK["v1"]], v)
                for j in range(HG):
                    hh = HG * g + j
                    mm = pe.matmul(ps_pv[32 * j:32 * j + 32, P * sbk:T],
                                   vx[par][:, sbk, D * hh:D * hh + D, :].rearrange("p d e -> p (d e)"),
                                   probs[sbk][:, j, :], start=(sbk == 0), stop=(sbk == TB - 1), skip_group_check=True)
                mm.then_inc(pv_done, 1)
            elif item == "mT":
                g = (s - 1) % NG
                lin_unit(pe, turn, s, item)
                if (v := turn.at(lambda n: NM * (NG * n + s))) is not None:
                    pe.wait_ge(max_done, v)
                pe.transpose(ps_lin[bank][0:HG * TB, 0:P], rowmax[:, g % 2, :], cst[:, 0, :]).then_inc(lin_full, 1)
            elif item[:2] == "eT":
                c = int(item[2])
                rows = P if c < EC - 1 else EL
                lin_unit(pe, turn, s, item)
                if (v := turn.at(lambda n: 16 * TB * (n + 1 + 1))) is not None:
                    pe.wait_ge(gathered, v)
                for tb in range(TB):
                    mm = pe.transpose(ps_lin[bank][0:rows, P * tb:P * tb + P], emb[:, tb, P * c:P * c + rows], cst[:, 0, :])
                mm.then_inc(lin_full, 1)
            elif item in ("h0", "h1"):
                u = int(item[1])
                lin_unit(pe, turn, s, item)
                if (v := turn.at(lambda n: out_of("eT2", n + 1))) is not None:
                    pe.wait_ge(lin_drained[LIN_BANK["eT2"]], v)
                for j in range(2):
                    tb = 2 * u + j
                    for c in range(EC):
                        rows = P if c < EC - 1 else EL
                        mm = pe.matmul(ps_lin[bank][:, C * j:C * j + C], embT[0:rows, c, P * tb:P * tb + P], wtok[0:rows, c, :],
                                       start=(c == 0), stop=(c == EC - 1))
                mm.then_inc(lin_full, 1)
            elif item[:2] == "xT" or item[:3] == "x2T":
                c = int(item[-1])
                first = item[:2] == "xT"
                off, src = (1, xn) if first else (-2, xn2)
                lin_unit(pe, turn, s, item)
                if (v := turn.at(lambda n: TB * (n + off + 1))) is not None:
                    pe.wait_ge(ln_out[0 if first else 1], v)
                for tb in range(TB):
                    mm = pe.transpose(ps_lin[bank][:, P * tb:P * tb + P], src[:, tb, P * c:P * c + P], cst[:, 0, :])
                mm.then_inc(lin_full, 1)
            elif item in ("q0", "k0", "q1", "k1"):
                c, col = int(item[1]), C * (item[0] == "k")
                lin_unit(pe, turn, s, item)
                if (v := turn.at(lambda n: out_of("xT1", n + 1))) is not None:
                    pe.wait_ge(lin_drained[LIN_BANK["xT1"]], v)
                products = [(w, x, k) for w, x in ((wqkv_hi, xT_hi), (wqkv_hi, xT_lo), (wqkv_lo, xT_hi)) for k in range(KC)]
                for j, (w, x, k) in enumerate(products):
                    mm = pe.matmul(ps_lin[bank][:], w[:, k, col + P * c:col + P * c + P], x[:, k, :],
                                   start=(j == 0), stop=(j == len(products) - 1))
                mm.then_inc(lin_full, 1)
            elif item in ("v0", "v1"):
                u = int(item[1])
                lin_unit(pe, turn, s, item)
                if (v := turn.at(lambda n: out_of("xT1", n + 1))) is not None:
                    pe.wait_ge(lin_drained[LIN_BANK["xT1"]], v)
                products = [(w, x, k) for w, x in ((wqkv_hi, xT_hi), (wqkv_hi, xT_lo), (wqkv_lo, xT_hi)) for k in range(KC)]
                for j in range(2):
                    tb = 2 * u + j
                    for m, (w, x, k) in enumerate(products):
                        mm = pe.matmul(ps_lin[bank][:, C * j:C * j + C], x[:, k, P * tb:P * tb + P], w[:, k, 2 * C:3 * C],
                                       start=(m == 0), stop=(m == len(products) - 1))
                mm.then_inc(lin_full, 1)
            elif item in ("pj0", "pj1", "r0", "r1", "kv0", "kv1"):
                u, kind = int(item[-1]), item[:-1]
                x, w = {"pj": (y[(turn.parity + 1) % 2], wp), "r": (mix_r, wr), "kv": (kact, wv)}[kind]
                lin_unit(pe, turn, s, item)
                if kind == "pj":
                    if (v := turn.at(lambda n: KC * (n - 1 + 1))) is not None:
                        pe.wait_ge(y_norm, v)
                elif kind == "r":
                    if (v := turn.at(lambda n: 2 * KC * (n - 2 + 1))) is not None:
                        pe.wait_ge(mix_step, v)
                else:
                    if (v := turn.at(lambda n: KC * (n - 2 + 1))) is not None:
                        pe.wait_ge(sq_done, v)
                for j in range(2):
                    tb = 2 * u + j
                    for k in range(KC):
                        mm = pe.matmul(ps_lin[bank][:, C * j:C * j + C], x[:, k, P * tb:P * tb + P], w[:, k, :],
                                       start=(k == 0), stop=(k == KC - 1))
                mm.then_inc(lin_full, 1)
            elif item in ("kk0", "kk1"):
                c = int(item[-1])
                lin_unit(pe, turn, s, item)
                if (v := turn.at(lambda n: 2 * KC * (n - 2 + 1))) is not None:
                    pe.wait_ge(mix_step, v)
                for k in range(KC):
                    mm = pe.matmul(ps_lin[bank][:], wk[:, k, P * c:P * c + P], mix_k[:, k, :], start=(k == 0), stop=(k == KC - 1))
                mm.then_inc(lin_full, 1)

        @block.tensor
        def _(pe):
            pe.wait_ge(s_load, 16 * NLOADS)
            pe.wait_ge(s_setup, SETUP_ONES)
            for k in range(KC):
                pe.matmul(ps_lin[0][:, 0:C], bvcol[:, k:k + 1].to_broadcast([P, P]), wp[:, k, :], start=(k == 0), stop=False)
            pe.matmul(ps_lin[0][:, 0:C], ones_row[:], bprow[:], start=False, stop=True).then_inc(s_bias_mm, 1)
            pe.wait_ge(s_ready, 1)
            for turn in turns(pe):
                for s in range(NG):
                    for item in STEPS[s]:
                        if turn.has(item, s) if item in BATCH or item in GROUP else False:
                            tensor_part(pe, turn, s, item)

        def full(engine, turn, item):
            if (v := turn.at(lambda n: lin(item, n + LIN_BATCH[item]))) is not None:
                engine.wait_ge(lin_full, v)

        def scalar_part(act, turn, s, item):
            bank = bank_of(s, item)
            if item[0] == "U":
                k = int(item[1:])
                sbk, heads = EXP_TILES[k]
                width = len(heads) * (T - P * sbk)
                if (v := turn.at(lambda n: NE * (NG * n + s - 2) + k + 1)) is not None:
                    act.wait_ge(exp_full, v)
                if (v := turn.at(lambda n: TB * (NG * n + s - 2 - 1) + sbk + 1)) is not None:
                    act.wait_ge(pv_done, v)
                act.activation(probs[sbk][:, heads[0]:heads[-1] + 1, :].rearrange("p h t -> p (h t)"),
                               ps_exp[:, k % EXP_BANKS, 0:width], ACT.Exp, scale=SCALE).then_inc(exp_done, 1)
            elif item == "PV3":
                g = (s - 3) % NG
                if (v := turn.at(lambda n: TB * (NG * n + s - 3 + 1))) is not None:
                    act.wait_ge(pv_done, v)
                if (v := turn.at(lambda n: 32 * ((NG * n + s - 3 - 2) // NG + 1))) is not None:
                    act.wait_ge(y_in[(g - 2) % NG], v)
                act.activation(y_raw[:, g % 2, :], ps_pv[:], ACT.Copy).then_inc(y_out, 1)
            elif item == "mT":
                g = (s - 1) % NG
                if (v := turn.at(lambda n: lin("mT", NG * n + s - 1))) is not None:
                    act.wait_ge(lin_full, v)
                if (v := turn.at(lambda n: 32 * ((NG * n + s - 1 - 2) // NG + 1))) is not None:
                    act.wait_ge(max_in[(g - 2) % NG], v)
                act.activation(maxT[:, g % 2, 0, :], ps_lin[bank][0:HG * TB, 0:P], ACT.Copy).then_inc(max_hi, 1)
            elif item[:2] == "eT":
                c = int(item[2])
                rows = P if c < EC - 1 else EL
                full(act, turn, item)
                if (v := turn.at(lambda n: lin("h1", n))) is not None:
                    act.wait_ge(lin_full, v)
                act.activation(embT[0:rows, c, :], ps_lin[bank][0:rows, :], ACT.Copy).then_inc(lin_drained[bank], 1)
            elif item[:2] == "xT":
                c = int(item[2])
                full(act, turn, item)
                if (v := turn.at(lambda n: max(lin("k1", n), lin("v1", n)))) is not None:
                    act.wait_ge(lin_full, v)
                act.activation(xT_hi[:, c, :], ps_lin[bank][:], ACT.Copy).then_inc(xT_hi_done, 1)
            elif item in ("q0", "k0", "q1", "k1"):
                c, j = int(item[1]), int(item[0] == "k")
                full(act, turn, item)
                if (v := turn.at(lambda n: 2 * (KC * (n + 1) + c - 1) + j + 1)) is not None:
                    act.wait_ge(split_lo, v)
                act.activation(raw[:, j, :], ps_lin[bank][:], ACT.Identity, bias=bqk[:, 2 * j + c:2 * j + c + 1]).then_inc(lin_drained[bank], 1)
            elif item in ("v0", "v1"):
                u = int(item[1])
                par = (turn.parity + 1) % 2
                full(act, turn, item)
                if (v := turn.at(lambda n: TB * NG * (n + 1 - 2 + 1))) is not None:
                    act.wait_ge(pv_done, v)
                act.activation(vx[par][:, 2 * u:2 * u + 2, :, 0], ps_lin[bank][:].rearrange("p (t c) -> p t c", t=2),
                               ACT.Copy).then_inc(lin_drained[bank], 1)
            elif item[:2] == "hi":
                c, j = int(item[2]), int(item[3])
                if (v := turn.at(lambda n: 2 * (KC * (n + 1) + c) + j + 1)) is not None:
                    act.wait_ge(rope_sum, v)
                for g in (2 * c, 2 * c + 1):
                    if (v := turn.at(lambda n: 16 * NSTACK * (n + 1))) is not None:
                        act.wait_ge(stack_in[g], v)
                act.activation(parts[0][:, c, j, :], raw[:, j, :], ACT.Copy).then_inc(split_hi, 1)
            elif item[:2] == "md":
                c, j = int(item[2]), int(item[3])
                if (v := turn.at(lambda n: 2 * (KC * (n + 1) + c) + j + 1)) is not None:
                    act.wait_ge(split_rest, v)
                act.activation(parts[1][:, c, j, :], raw[:, j, :], ACT.Copy).then_inc(split_mid, 1)
            elif item in ("h0", "h1"):
                u = int(item[1])
                full(act, turn, item)
                if (v := turn.at(lambda n: 2 * (n + 1))) is not None:
                    act.wait_ge(hb_done, v)
                if (v := turn.at(lambda n: TB * (n + 1))) is not None:
                    act.wait_ge(ln_out[0], v)
                act.activation(h[:, 2 * u:2 * u + 2, :], ps_lin[bank][:].rearrange("p (t c) -> p t c", t=2),
                               ACT.Copy).then_inc(lin_drained[bank], 1)
            elif item in ("sq0", "sq1"):
                c = int(item[2])
                if (v := turn.at(lambda n: out_of(f"kk{c}", n - 2))) is not None:
                    act.wait_ge(lin_drained[LIN_BANK[f"kk{c}"]], v)
                act.activation(kact[:, c, :], kact[:, c, :], ACT.Square).then_inc(sq_done, 1)
            elif item in ("x2T0", "x2T1"):
                c = int(item[3])
                full(act, turn, item)
                if (v := turn.at(lambda n: 2 * KC * (n - 2))) is not None:
                    act.wait_ge(mix_step, v)
                act.activation(x2T[:, c, 1:T + 1], ps_lin[bank][:], ACT.Copy).then_inc(lin_drained[bank], 1)
            elif item in ("kk0", "kk1"):
                c = int(item[2])
                full(act, turn, item)
                if (v := turn.at(lambda n: lin("kv1", n - 3))) is not None:
                    act.wait_ge(lin_full, v)
                act.activation(kact[:, c, :], ps_lin[bank][:], ACT.Relu).then_inc(lin_drained[bank], 1)
            elif item in ("r0", "r1"):
                u = int(item[1])
                full(act, turn, item)
                if (v := turn.at(lambda n: 16 * (n - 2))) is not None:
                    act.wait_ge(stored, v)
                act.activation(gate[:, 2 * u:2 * u + 2, :], ps_lin[bank][:].rearrange("p (t c) -> p t c", t=2),
                               ACT.Tanh, scale=0.5).then_inc(lin_drained[bank], 1)

        @block.scalar
        def _(act):
            act.wait_ge(s_load, 16 * NLOADS)
            act.wait_ge(s_ready, 1)
            for turn in turns(act):
                for s in range(NG):
                    for item in STEPS[s]:
                        if turn.has(item, s) if item in BATCH or item in GROUP else False:
                            scalar_part(act, turn, s, item)

        def ln_stats(dve, turn, j, x, off, half, unit):
            if (v := turn.at(lambda n: out_of(unit, n + off))) is not None:
                dve.wait_ge(lin_drained[LIN_BANK[unit]], v)
            for tb in (2 * half, 2 * half + 1):
                dve.bn_stats(ln[j]["stats"][:, tb, :], x[:, tb, :]).then_inc(ln_step[j], 1)

        def ln_variance(dve, turn, j, off):
            a = ln[j]
            if (v := turn.at(lambda n: 9 * (n + off) + TB)) is not None:
                dve.wait_ge(ln_step[j], v)
                dve.sem_inc(passed["dve"], 1)
            if (v := turn.at(lambda n: TB * (n + off))) is not None:
                dve.wait_ge(ln_out[j], v)
                dve.sem_inc(passed["dve"], 1)
            for tb in range(TB):
                dve.bn_aggr(a["mv"][:, tb, :], a["stats"][:, tb, :]).then_inc(ln_step[j], 1)
            if (v := turn.at(lambda n: 9 * (n + off) + 2 * TB)) is not None:
                dve.wait_ge(ln_step[j], v)
            dve.tensor_scalar(a["var"][:], a["mv"][:, :, 1], EPS, None, ALU.add).then_inc(ln_step[j], 1)

        def ln_normalise(dve, turn, j, x, to, off, half, reader):
            a = ln[j]
            if (v := turn.at(lambda n: n + off + 1)) is not None:
                dve.wait_ge(ln_rstd[j], v)
            if (v := turn.at(lambda n: lin(reader, n + off - 1))) is not None:
                dve.wait_ge(lin_full, v)
            for tb in (2 * half, 2 * half + 1):
                dve.tensor_scalar(to[:, tb, :], x[:, tb, :], a["mv"][:, tb, 0:1], a["rstd"][:, tb:tb + 1],
                                  ALU.subtract, ALU.mult).then_inc(ln_out[j], 1)

        def vector_part(dve, turn, s, item):
            bank = bank_of(s, item)
            if item[0] == "M":
                k = int(item[1:])
                tb, heads = MAX_TILES[k]
                slot = (s + k) % 2
                width = P * (tb + 1)
                if (v := turn.at(lambda n: NM * (NG * n + s) + k + 1)) is not None:
                    dve.wait_ge(max_full, v)
                src = ps_max[:, slot, 0:width * len(heads)].rearrange("p (h t) -> p h t", h=len(heads))
                dst = rowmax[:, s % 2, :].rearrange("p (h t) -> p h t", h=HG)[:, heads[0]:heads[-1] + 1, tb]
                dve.tensor_reduce(dst, src, AX.X, ALU.max).then_inc(max_done, 1)
            elif item == "mT":
                g = (s - 1) % NG
                if (v := turn.at(lambda n: NG * n + s - 1 + 1)) is not None:
                    dve.wait_ge(max_hi, v)
                dve.tensor_tensor(maxT[:, g % 2, 1, :], ps_lin[bank][0:HG * TB, 0:P], maxT[:, g % 2, 0, :],
                                  ALU.subtract).then_inc(lin_drained[bank], 1)
            elif item == "idx":
                if (v := turn.at(lambda n: 16 * (n + 2 + 1))) is not None:
                    dve.wait_ge(ids_in, v)
                dve.tensor_scalar(row_t[:], ids_sb[:], 1.0, 0.0, ALU.add, ALU.max).then_inc(rows_done, 1)
                if (v := turn.at(lambda n: 2 * (n + 2) + 1)) is not None:
                    dve.wait_ge(rows_done, v)
                if (v := turn.at(lambda n: 16 * TB * (n + 2))) is not None:
                    dve.wait_ge(gathered, v)
                dve.tensor_scalar(row_id[:], row_t[:], float(ROWS + 1), None, ALU.min).then_inc(rows_done, 1)
            elif item in ("ln1a0", "ln1a1"):
                ln_stats(dve, turn, 0, h, 1, int(item[-1]), f"h{item[-1]}")
            elif item == "ln1v":
                ln_variance(dve, turn, 0, 1)
            elif item in ("ln1n0", "ln1n1"):
                ln_normalise(dve, turn, 0, h, xn, 1, int(item[-1]), "xT1")
            elif item in ("ln2a0", "ln2a1"):
                ln_stats(dve, turn, 1, h1, -1, int(item[-1]), f"pj{item[-1]}")
            elif item == "ln2v":
                ln_variance(dve, turn, 1, -1)
            elif item in ("ln2n0", "ln2n1"):
                ln_normalise(dve, turn, 1, h1, xn2, -1, int(item[-1]), "x2T1")
            elif item in ("xT0", "xT1"):
                c = int(item[2])
                if (v := turn.at(lambda n: KC * (n + 1) + c + 1)) is not None:
                    dve.wait_ge(xT_hi_done, v)
                dve.tensor_tensor(xT_lo[:, c, :], ps_lin[bank][:], xT_hi[:, c, :].bitcast(F32), ALU.subtract).then_inc(lin_drained[bank], 1)
            elif item[:2] == "tt":
                c, j = int(item[2]), int(item[3])
                if (v := turn.at(lambda n: 2 * (KC * (n + 1) + c) + j + 1)) is not None:
                    dve.wait_ge(split_hi, v)
                dve.tensor_tensor(raw[:, j, :], raw[:, j, :], parts[0][:, c, j, :], ALU.subtract).then_inc(split_rest, 1)
            elif item[:2] == "lo":
                c, j = int(item[2]), int(item[3])
                if (v := turn.at(lambda n: 2 * (KC * (n + 1) + c) + j + 1)) is not None:
                    dve.wait_ge(split_mid, v)
                dve.tensor_tensor(parts[2][:, c, j, :], raw[:, j, :], parts[1][:, c, j, :], ALU.subtract).then_inc(split_lo, 1)
            elif item == "rc":
                g = (s - 3) % NG
                if (v := turn.at(lambda n: 32 * ((NG * n + s - 3) // NG + 1))) is not None:
                    dve.wait_ge(y_in[g], v)
                if (v := turn.at(lambda n: 16 * ((NG * n + s - 3) // NG))) is not None:
                    dve.wait_ge(inv_out[g], v)
                dve.reciprocal(inv_sums[:, g, :], sums[:, g, :]).then_inc(inv_done, 1)
            elif item in ("yn0", "yn1"):
                c = int(item[2])
                for g in (2 * c, 2 * c + 1):
                    if (v := turn.at(lambda n: 32 * (n - 1 + 1))) is not None:
                        dve.wait_ge(y_in[g], v)
                    if (v := turn.at(lambda n: 16 * (n - 1 + 1))) is not None:
                        dve.wait_ge(inv_in[g], v)
                yb = y[(turn.parity + 1) % 2][:, c, :]
                dve.tensor_tensor(yb, yb, inv_rows[:, c, :], ALU.mult).then_inc(y_norm, 1)
            elif item in ("pj0", "pj1"):
                u = int(item[2])
                par = (turn.parity + 1) % 2
                full(dve, turn, item)
                if (v := turn.at(lambda n: 2 * (n - 1 + 1))) is not None:
                    dve.wait_ge(hb_done, v)
                if (v := turn.at(lambda n: TB * (n - 1))) is not None:
                    dve.wait_ge(ln_out[1], v)
                if (v := turn.at(lambda n: 2 * (n - 1))) is not None:
                    dve.wait_ge(fin_done, v)
                dve.tensor_tensor(h1[:, 2 * u:2 * u + 2, :], ps_lin[bank][:].rearrange("p (t c) -> p t c", t=2),
                                  hb[par][:, 2 * u:2 * u + 2, :], ALU.add).then_inc(lin_drained[bank], 1)
            elif item in ("mm0", "mm1"):
                c = int(item[2])
                before = x2T[:, c, 0:T]
                if (v := turn.at(lambda n: KC * (n - 2) + c + 1)) is not None:
                    dve.wait_ge(mix_diff, v)
                if (v := turn.at(lambda n: lin("r1", n - 3))) is not None:
                    dve.wait_ge(lin_full, v)
                dve.scalar_tensor_tensor(out=mix_r[:, c, :], in0=mix_k[:, c, :], scalar=muc[:, 0, c:c + 1], in1=before,
                                         op0=ALU.mult, op1=ALU.add).then_inc(mix_step, 1)
                if (v := turn.at(lambda n: 2 * (KC * (n - 2) + c) + 1)) is not None:
                    dve.wait_ge(mix_step, v)
                dve.scalar_tensor_tensor(out=mix_k[:, c, :], in0=mix_k[:, c, :], scalar=muc[:, 1, c:c + 1], in1=before,
                                         op0=ALU.mult, op1=ALU.add).then_inc(mix_step, 1)
            elif item in ("kv0", "kv1"):
                u = int(item[2])
                full(dve, turn, item)
                if (v := turn.at(lambda n: out_of("r1", n - 2))) is not None:
                    dve.wait_ge(lin_drained[LIN_BANK["r1"]], v)
                half = gate[:, 2 * u:2 * u + 2, :]
                dve.scalar_tensor_tensor(out=half, in0=half, scalar=1.0, in1=ps_lin[bank][:].rearrange("p (t c) -> p t c", t=2),
                                         op0=ALU.add, op1=ALU.mult).then_inc(lin_drained[bank], 1)
            elif item in ("fin0", "fin1"):
                u = int(item[3])
                if (v := turn.at(lambda n: out_of(f"kv{u}", n - 2))) is not None:
                    dve.wait_ge(lin_drained[LIN_BANK[f"kv{u}"]], v)
                half = gate[:, 2 * u:2 * u + 2, :]
                dve.scalar_tensor_tensor(out=half, in0=half, scalar=0.5, in1=h1[:, 2 * u:2 * u + 2, :], op0=ALU.mult,
                                         op1=ALU.add).then_inc(fin_done, 1)

        @block.vector
        def _(dve):
            dve.memset(ones_row[:], 1.0).then_inc(s_setup, 1)
            dve.memset(minus_half[:], -0.5)
            for v in vx:
                dve.memset(v[:, :, :, 1], 1.0)
            dve.memset(x2T[:, :, 0:1], 0.0)
            dve.memset(ks[KS:KM, :, :], -1.0)
            dve.wait_ge(s_load, 16 * NLOADS)
            dve.tensor_copy(ident_bf[:], cst[:, 0, :])
            dve.tensor_copy(mask_bf[:], cst[:, 1, :])
            dve.tensor_copy(wqkv_hi[:], stage).then_inc(s_setup, 1)
            dve.wait_ge(s_setup, 2)
            dve.tensor_tensor(wqkv_lo[:], stage, wqkv_hi[:].bitcast(F32), ALU.subtract)
            dve.wait_ge(s_bias_mm, 1)
            dve.tensor_copy(bias_p[:], ps_lin[0][:, 0:C]).then_inc(s_ready, 1)
            for turn in turns(dve):
                for s in range(NG):
                    for item in STEPS[s]:
                        if turn.has(item, s) if item in BATCH or item in GROUP else False:
                            vector_part(dve, turn, s, item)

        def gpsimd_part(pool, turn, s, item):
            if item[0] == "U":
                k = int(item[1:])
                if k + 1 not in EXP_TILES_UPTO:
                    return
                sbk = EXP_TILES_UPTO.index(k + 1)
                if (v := turn.at(lambda n: NE * (NG * n + s - 2) + k + 1)) is not None:
                    pool.wait_ge(exp_done, v)
                    pool.sem_inc(passed["pool"], 1)
                diag = probs[sbk][:, :, 0:P]
                pool.affine_select(out=diag, in_=diag, compare_op=ALU.is_ge, fill=0.0, base=0,
                                   pattern=[[0, HG], [1, P]], channel_multiplier=-1).then_inc(masked, 1)
            elif item == "gather":
                if (v := turn.at(lambda n: 2 * (n + 2 + 1))) is not None:
                    pool.wait_ge(rows_done, v)
                if (v := turn.at(lambda n: lin("eT2", n + 1))) is not None:
                    pool.wait_ge(lin_full, v)
                    pool.sem_inc(passed["pool"], 1)
                for tb in range(TB):
                    pool.indirect_dma_start(out=emb[:, tb, :], out_offset=None, in_=table,
                                            in_offset=bass.IndirectOffsetOnAxis(ap=row_id[:, tb:tb + 1], axis=0)
                                            ).then_inc(gathered, 16)
            elif item in ("ln1p", "ln2p"):
                j = int(item[2]) - 1
                off = BATCH[item]
                if (v := turn.at(lambda n: 9 * (n + off + 1))) is not None:
                    pool.wait_ge(ln_step[j], v)
                if (v := turn.at(lambda n: TB * (n + off))) is not None:
                    pool.wait_ge(ln_out[j], v)
                pool.tensor_tensor(ln[j]["rstd"][:], ln[j]["var"][:], minus_half[:], ALU.pow).then_inc(ln_rstd[j], 1)
            elif item[:4] == "rcos":
                c, j = int(item[4]), int(item[5])
                if (v := turn.at(lambda n: 64 * (n + 1 + 1))) is not None:
                    pool.wait_ge(swap_in[c], v)
                pool.tensor_tensor(raw[:, j, :], raw[:, j, :], rope[:, 0, :], ALU.mult).then_inc(rope_cos, 1)
            elif item[:4] == "rsin":
                c, j = int(item[4]), int(item[5])
                if (v := turn.at(lambda n: 64 * (n + 1 + 1))) is not None:
                    pool.wait_ge(swap_in[c], v)
                pool.tensor_tensor(swapped[:, j, :], swapped[:, j, :], rope[:, 1, :], ALU.mult).then_inc(rope_sin, 1)
            elif item[:4] == "radd":
                c, j = int(item[4]), int(item[5])
                if (v := turn.at(lambda n: 2 * (KC * (n + 1) + c) + j + 1)) is not None:
                    pool.wait_ge(rope_cos, v)
                if (v := turn.at(lambda n: 2 * (KC * (n + 1) + c) + j + 1)) is not None:
                    pool.wait_ge(rope_sin, v)
                pool.tensor_tensor(raw[:, j, :], raw[:, j, :], swapped[:, j, :], ALU.add).then_inc(rope_sum, 1)
            elif item in ("mix0", "mix1"):
                c = int(item[3])
                x, before = x2T[:, c, 1:T + 1], x2T[:, c, 0:T]
                if (v := turn.at(lambda n: out_of(f"x2T{c}", n - 2))) is not None:
                    pool.wait_ge(lin_drained[LIN_BANK[f"x2T{c}"]], v)
                if (v := turn.at(lambda n: lin("kk1", n - 3))) is not None:
                    pool.wait_ge(lin_full, v)
                pool.tensor_tensor(mix_k[:, c, :], x, before, ALU.subtract).then_inc(mix_diff, 1)
            elif item in ("hb0", "hb1"):
                u = int(item[2])
                par = (turn.parity + 1) % 2
                if (v := turn.at(lambda n: out_of(f"h{u}", n + 1))) is not None:
                    pool.wait_ge(lin_drained[LIN_BANK[f"h{u}"]], v)
                if (v := turn.at(lambda n: out_of("pj1", n - 1))) is not None:
                    pool.wait_ge(lin_drained[LIN_BANK["pj1"]], v)
                pool.tensor_tensor(hb[par][:, 2 * u:2 * u + 2, :], h[:, 2 * u:2 * u + 2, :],
                                   bias_p[:].unsqueeze(1).to_broadcast([P, 2, C]), ALU.add).then_inc(hb_done, 1)

        @block.gpsimd
        def _(pool):
            pool.wait_ge(s_load, 16 * NLOADS)
            pool.wait_ge(s_ready, 1)
            for turn in turns(pool):
                for s in range(NG):
                    for item in STEPS[s]:
                        if turn.has(item, s) if item in BATCH or item in GROUP else False:
                            gpsimd_part(pool, turn, s, item)

NLOADS = 13
SETUP_ONES = 1


def kernel(**inputs):
    import concourse.bacc as bacc
    from concourse.bass_utils import run_bass_kernel_spmd

    def arr(name):
        return np.ascontiguousarray(inputs[name])

    f = np.float32
    ids = np.ascontiguousarray(arr("x").reshape(B, TB, P).transpose(0, 2, 1))
    t0, t1, t2 = arr("L0_tok_t0"), arr("L0_tok_t1"), arr("L0_tok_t2")
    table = np.zeros((ROWS + 2, EW), f)
    r1, r2 = 1 + len(t0), 1 + len(t0) + len(t1)
    table[1:r1, 0:E0] = t0
    table[r1:r2, E0:E0 + E1] = t1
    table[r2:r2 + len(t2), E0 + E1:EW] = t2
    w_tok = np.concatenate([arr("L0_tok_w0"), arr("L0_tok_w1"), arr("L0_tok_w2")], axis=0)
    order = np.arange(C).reshape(KC, 2, HG, D).transpose(0, 1, 3, 2).reshape(-1)
    w_qkv = np.concatenate([arr("L0_attn_wq").T[:, order], arr("L0_attn_wk").T[:, order], arr("L0_attn_wv").T], axis=1)
    b_qk = np.concatenate([arr("L0_attn_bq")[order].reshape(KC, P), arr("L0_attn_bk")[order].reshape(KC, P)]).T
    b_v = arr("L0_attn_bv").reshape(KC, P).T
    mu = np.stack([arr("L0_ffn_mu_r").reshape(KC, P).T, arr("L0_ffn_mu_k").reshape(KC, P).T], axis=1)
    half = D // 2
    i = np.arange(half, dtype=f)
    alpha = (f(1.0) / np.power(f(10000.0), f(2.0) * i / f(D))).astype(f)
    ang = (np.arange(T, dtype=f)[:, None] * alpha).astype(f)
    d_of = (np.arange(P) // HG) % D
    cos = np.cos(ang).astype(f).T[d_of % half]
    sin = np.sin(ang).astype(f).T[d_of % half] * np.where(d_of < half, f(-1), f(1))[:, None]
    cos_sin = np.stack([cos, sin], axis=1).astype(f)
    consts = np.stack([np.eye(P, dtype=f), np.triu(np.full((P, P), MASKED, f), 1)], axis=1)
    arrays = dict(ids=ids, table=table, w_tok=w_tok, w_qkv=w_qkv, b_qk=b_qk, w_p=arr("L0_attn_wp").T, b_v=b_v,
                  b_p=arr("L0_attn_bp").reshape(1, C), w_r=arr("L0_ffn_W_r").T, w_k=arr("L0_ffn_W_k").T,
                  w_v=arr("L0_ffn_W_v").T, mu=mu, cos_sin=cos_sin, consts=consts)
    arrays = {name: np.ascontiguousarray(a) for name, a in arrays.items()}

    nc = bacc.Bacc("TRN2", target_bir_lowering=False, num_devices=1)
    args = {name: nc.dram_tensor(f"in_{name}", a.shape, mybir.dt.from_np(a.dtype), kind="ExternalInput").ap()
            for name, a in arrays.items()}
    out = nc.dram_tensor("out_h", (B, T, C), F32, kind="ExternalOutput").ap()
    tower(nc, out=out.rearrange("b (k p) c -> b p k c", p=P), **args)
    r = run_bass_kernel_spmd(nc, [{f"in_{name}": a for name, a in arrays.items()}], core_ids=[0])
    return r.results[0]["out_h"]
```

```python
from contextlib import ExitStack

import concourse.bass as bass
import numpy as np
from concourse import mybir

ALU = mybir.AluOpType
ACT = mybir.ActivationFunctionType
AX = mybir.AxisListType
F32, F32R, BF16, I32, U32 = (mybir.dt.float32, mybir.dt.float32r, mybir.dt.bfloat16, mybir.dt.int32,
                             mybir.dt.uint32)

P = 128
B, T, C, H = 32, 512, 256, 16
D = C // H
TB = T // P
KC = C // P
HG = 4
NG = H // HG
HC = H // KC
E0, E1, E2 = 256, 64, 16
EW = E0 + E1 + E2
EC = (EW + P - 1) // P
EL = EW - (EC - 1) * P
ROWS = 25000
NPART = 3
NCOMB = 6
Q_PART = (0, 1, 2, 0, 1, 0)
K_PART = (0, 0, 0, 1, 1, 2)
KS = NCOMB * D
KM = KS + 2
SCALE = float(D) ** -0.5
EPS = 1e-5
MASKED = -1e30

MAX_TILES = ([(3, (h,)) for h in range(HG)] + [(2, (h,)) for h in range(HG)]
             + [(1, (0, 1)), (1, (2, 3)), (0, (0, 1, 2, 3))])
NM = len(MAX_TILES)
EXP_TILES = ([(0, (h,)) for h in range(HG)] + [(1, (h,)) for h in range(HG)]
             + [(2, (0, 1)), (2, (2, 3)), (3, (0, 1, 2, 3))])
NE = len(EXP_TILES)
EXP_BANKS = 3
EXP_TILES_UPTO = tuple(max(k for k, (sb, _) in enumerate(EXP_TILES) if sb == b) + 1 for b in range(TB))

STEPS = [" ".join(lines).split() for lines in (
    [
        "eT0 eT1 M0 PV2 xload eT2 mT M1 idx PV3 x2T0 M2 h0 M3 M4 U0 mm0 rc U1 mix0 gather ln1a0 U2 h1 M5 U3",
        "M6 ln1a1 U4 U5 M7 U6 M8 U7 x2T1 ro U8 rb ln1p mix1 U9 ln1v U10 M9 M10 ln1n0 PV0 PV1",
    ],
    [
        "st10 ln1n1 mT st11 M0 M1 xT0 mrl0 xT1 mm1 PV2 mrh0 M2 mrh1 PV3 sw0 M3 q0 st12 k0 M4 U0 U1 mrl1 M5 U2",
        "r0 U3 U4 rc U5 M6 rcos00 M7 mkh0 r1 mkl0 U6 PV0 ro M8 U7 mkh1 M9 mkl1 U8 U9 rb M10 yn0 U10 PV1",
    ],
    [
        "mT v0 M0 rsin00 kk0 M1 sq0 rcos01 radd00 PV2 rsin01 PV3 M2 M3 U0 U1 U2 radd01 hi00 kk1 M4 U3 ro M5",
        "U4 hi01 kal0 v1 rb md00 rc md01 kah0 tt00 U5 tt01 M6 U6 lo00 U7 q1 sw1 M7 lo01 k1 M8 st00 U8 sq1 M9",
        "U9 U10 yn1 PV0 M10 PV1",
    ],
    [
        "M0 kah1 M1 PV2 yh0 kal1 mT yl0 yh1 rcos10 PV3 M2 M3 kv0 M4 yl1 rcos11 M5 st01 fin0 kv1 rsin10 M6",
        "radd10 fin1 M7 st02 rsin11 out pj0 U0 U1 M8 U2 U3 ln2a0 ro pj1 rb U4 radd11 U5 rc U6 ln2a1 hi10 U7",
        "M9 ln2p ln2v U8 tt10 hi11 U9 M10 tt11 md10 PV0 hb0 PV1 U10 ln2n0 lo10 md11 ln2n1 lo11 hb1",
    ],
)]
LIN_BATCH = {"eT0": 1, "eT1": 1, "eT2": 1, "h0": 1, "h1": 1, "xT0": 1, "xT1": 1, "q0": 1, "k0": 1,
             "q1": 1, "k1": 1, "v0": 1, "v1": 1, "pj0": -1, "pj1": -1, "x2T0": -2, "x2T1": -2,
             "kk0": -2, "kk1": -2, "r0": -2, "r1": -2, "kv0": -2, "kv1": -2}
BATCH = dict(LIN_BATCH, xload=2, idx=2, gather=2, ln1a0=1, ln1a1=1, ln1v=1, ln1p=1, ln1n0=1, ln1n1=1, sw0=1, sw1=1,
             hb0=1, hb1=1, yn0=-1, yn1=-1, ln2a0=-1, ln2a1=-1, ln2v=-1, ln2p=-1,
             ln2n0=-1, ln2n1=-1, mix0=-2, mix1=-2, mm0=-2, mm1=-2, sq0=-2, sq1=-2, fin0=-2, fin1=-2, out=-2)
BATCH.update({f"st{c}{third}": 1 if c == 0 else 0 for c in range(KC) for third in range(3)})
BATCH.update({f"{x}{part}{c}": -1 if x == "y" else -2 for x in ("y", "mr", "mk", "ka") for part in ("h", "l") for c in range(KC)})
BATCH.update({f"{step}{c}{j}": 1 for step in ("rcos", "rsin", "radd", "hi", "tt", "md", "lo") for c in range(KC) for j in range(2)})
GROUP = {"mT": -1, "rc": -2, "ro": -2, "rb": -2, "PV0": -1, "PV1": -1, "PV2": -2, "PV3": -2}
GROUP.update({f"U{k}": -1 for k in range(NE)})
GROUP.update({f"M{k}": 0 for k in range(NM)})

NLOADS = 13
SETUP_ONES = 1
FIRST_N, LAST_N = -2, B + 1
LOOP_FROM, LOOP_TO = 4, 30


def batch_ok(b):
    return 0 <= b < B


def lin_units(n):
    position = 0
    for s in range(NG):
        for item in STEPS[s]:
            if item in LIN_BATCH or item == "mT":
                key = n + LIN_BATCH[item] if item in LIN_BATCH else NG * n + s - 1
                if 0 <= key < (B if item in LIN_BATCH else NG * B):
                    yield item, key, position % 2
                position += 1


def count_lin_units():
    seen, in_bank, n_units, n_bank = {}, {}, 0, [0, 0]
    for n in range(FIRST_N, LAST_N + 1):
        for item, key, bank in lin_units(n):
            n_units += 1
            n_bank[bank] += 1
            seen[item, key], in_bank[item, key] = n_units, n_bank[bank]
    return seen, in_bank


LIN, LIN_IN_BANK = count_lin_units()
LIN_BANK = {item if item != "mT" else (item, (key + 1) % NG): bank for item, key, bank in lin_units(4)}


class Turn:

    def __init__(self, n=None, register=None, offset=0):
        self.register, self.offset = register, offset
        self.ns = [n] if register is None else list(range(LOOP_FROM + offset, LOOP_TO + offset, 2))
        self.parity = self.ns[0] % 2

    def has(self, item, s):
        def ok(n):
            if item in GROUP:
                return 0 <= NG * n + s + GROUP[item] < NG * B
            return batch_ok(n + BATCH[item])
        return all(ok(n) for n in self.ns)

    def at(self, count):
        if all(count(n) <= 0 for n in self.ns):
            return None
        return self.value(count)

    def value(self, count):
        vs = [count(n) for n in self.ns]
        if self.register is None:
            return vs[0]
        slope = (vs[-1] - vs[0]) // (self.ns[-1] - self.ns[0])
        assert all(v == vs[0] + slope * (n - self.ns[0]) for v, n in zip(vs, self.ns)) and vs[0] > 0
        return self.register * slope + (vs[0] - slope * (self.ns[0] - self.offset))


def turns(engine):
    for n in range(FIRST_N, LOOP_FROM):
        yield Turn(n)
    with engine.Fori(LOOP_FROM, LOOP_TO - 1, 2) as register:
        for offset in range(2):
            yield Turn(register=register, offset=offset)
    for n in range(LOOP_TO, LAST_N + 1):
        yield Turn(n)


def bank_of(item, s=None):
    return LIN_BANK.get((item, s) if item == "mT" else item)


def lin(unit, key):
    return LIN.get((unit, key), 0)


def out_of(unit, key):
    return LIN_IN_BANK.get((unit, key), 0)


def tower(nc, ids, table, w_tok, w_qkv, b_qk, w_p, b_v, b_p, w_r, w_k, w_v, mu, cos_sin, consts, out):
    with ExitStack() as ctx:
        def sb(name, shape, dt=F32):
            return ctx.enter_context(nc.sbuf_tensor(name, shape, dt))

        def psum(name, shape):
            return ctx.enter_context(nc.psum_tensor(name, shape, F32))

        def sem(name):
            return ctx.enter_context(nc.semaphore(name))

        ps_exp = psum("ps_exp", [P, EXP_BANKS, T])
        ps_max = psum("ps_max", [P, 2, T])
        ps_pv = psum("ps_pv", [P, T])
        ps_lin = [psum(f"ps_lin{j}", [P, T]) for j in range(2)]

        wtok = sb("wtok", [P, EC, C])
        wqkv_hi = sb("wqkv_hi", [P, KC, 3 * C], F32R)
        wqkv_lo = sb("wqkv_lo", [P, KC, 3 * C], F32R)
        wp_hi, wr_hi, wk_hi, wv_hi = (sb(f"{w}_hi", [P, KC, C], F32R) for w in ("wp", "wr", "wk", "wv"))
        wp_lo, wr_lo, wk_lo, wv_lo = (sb(f"{w}_lo", [P, KC, C], F32R) for w in ("wp", "wr", "wk", "wv"))
        bqk = sb("bqk", [P, 4])
        bvcol = sb("bvcol", [P, KC])
        bprow = sb("bprow", [1, C])
        ones_row = sb("ones_row", [1, P])
        bias_p = sb("bias_p", [P, C])
        muc = sb("muc", [P, 2, KC])
        rope = sb("rope", [P, 2, T])
        cst = sb("cst", [P, 2, P])
        ident_bf = sb("ident_bf", [P, P], BF16)
        mask_bf = sb("mask_bf", [P, P], BF16)
        minus_half = sb("minus_half", [P, TB])
        ids_sb = sb("ids_sb", [P, TB], I32)
        row_t = sb("row_t", [P, TB], I32)
        row_id = sb("row_id", [P, TB], U32)
        emb = sb("emb", [P, TB, EW])
        embT = sb("embT", [P, EC, T])
        h = sb("h", [P, TB, C])
        xn = sb("xn", [P, TB, C])
        xy_hi = sb("xy_hi", [P, KC, T], F32R)
        xy_lo = sb("xy_lo", [P, KC, T], F32R)
        raw = sb("raw", [P, 2, T])
        swapped = sb("swapped", [P, 2, T])
        parts = [sb(f"part{j}", [P, KC, 2, T], BF16) for j in range(NPART)]
        qs = sb("qs", [KM, H, T], BF16)
        ks = sb("ks", [KM, H, T], BF16)
        vx = [sb(f"vx{p}", [P, TB, C, 2]) for p in range(2)]
        probs = [sb(f"probs{j}", [P, HG, T - P * j]) for j in range(TB)]
        rowmax = sb("rowmax", [P, 2, HG * TB])
        maxT = sb("maxT", [HG * TB, 2, 2, P], BF16)
        y_raw = sb("y_raw", [P, T])
        y = [sb(f"y{p}", [P, KC, T]) for p in range(2)]
        sums = sb("sums", [P, NG, HG * T // P])
        inv_sums = sb("inv_sums", [P, NG, HG * T // P])
        inv_rows = sb("inv_rows", [P, KC, T])
        hb = [sb(f"hb{p}", [P, TB, C]) for p in range(2)]
        h1 = sb("h1", [P, TB, C])
        x2T = sb("x2T", [P, KC, T + 1])
        mix_r = sb("mix_r", [P, KC, T])
        mix_k = sb("mix_k", [P, KC, T])
        kact = mix_r
        mix_hi = sb("mix_hi", [P, KC, T], F32R)
        mix_lo = sb("mix_lo", [P, KC, T], F32R)
        gate = sb("gate", [P, TB, C])
        ln = [dict(stats=sb(f"ln_stats{j}", [P, TB, 6]), mv=sb(f"ln_mv{j}", [P, TB, 2]),
                   var=sb(f"ln_var{j}", [P, TB]), rstd=sb(f"ln_rstd{j}", [P, TB])) for j in range(2)]
        inv_dram = nc.dram_tensor("inv_dram", [NG, HG, T], F32, kind="Internal").ap()

        s_load = sem("s_load")
        s_setup = sem("s_setup")
        s_bias_mm = sem("s_bias_mm")
        s_ready = sem("s_ready")
        lin_full = sem("lin_full")
        lin_drained = [sem(f"lin_drained{j}") for j in range(2)]
        ids_in = sem("ids_in")
        rows_done = sem("rows_done")
        gathered = sem("gathered")
        ln_step = [sem(f"ln{j}_step") for j in range(2)]
        ln_rstd = [sem(f"ln{j}_rstd") for j in range(2)]
        ln_out = [sem(f"ln{j}_out") for j in range(2)]
        xT_hi_done = sem("xT_hi_done")
        swap_in = [sem(f"swap_in{c}") for c in range(KC)]
        rope_cos = sem("rope_cos")
        rope_sin = sem("rope_sin")
        rope_sum = sem("rope_sum")
        split_hi = sem("split_hi")
        split_rest = sem("split_rest")
        split_mid = sem("split_mid")
        split_lo = sem("split_lo")
        stack_in = [sem(f"stack_in{c}") for c in range(KC)]
        max_full = sem("max_full")
        max_done = sem("max_done")
        max_hi = sem("max_hi")
        max_in = [sem(f"max_in{g}") for g in range(NG)]
        exp_full = sem("exp_full")
        exp_done = sem("exp_done")
        masked = sem("masked")
        pv_done = sem("pv_done")
        y_out = sem("y_out")
        y_in = [sem(f"y_in{g}") for g in range(NG)]
        inv_done = sem("inv_done")
        inv_out = [sem(f"inv_out{g}") for g in range(NG)]
        inv_in = [sem(f"inv_in{g}") for g in range(NG)]
        y_norm = sem("y_norm")
        hb_done = sem("hb_done")
        mix_diff = sem("mix_diff")
        mix_step = sem("mix_step")
        sq_done = sem("sq_done")
        s_split_hi = sem("s_split_hi")
        s_split = sem("s_split")
        hi_done = {x: sem(f"{x}_hi_done") for x in ("y", "mr", "mk", "ka")}
        lo_done = {x: sem(f"{x}_lo_done") for x in ("y", "mr", "mk", "ka")}
        fin_done = sem("fin_done")
        stored = sem("stored")

        passed = {e: sem(f"passed_{e}") for e in ("sp", "dve", "pool")}
        NSTACK = 2 * NCOMB
        stage = probs[0].rearrange("p a b -> p (a b)")[:, 0:KC * 3 * C].rearrange("p (k c) -> p k c", k=KC)
        flat = probs[1].rearrange("p a b -> p (a b)")
        wp, wr, wk = (flat[:, j * KC * C:(j + 1) * KC * C].rearrange("p (k c) -> p k c", k=KC) for j in range(3))
        wv = probs[2].rearrange("p a b -> p (a b)")[:, 0:KC * C].rearrange("p (k c) -> p k c", k=KC)
        block = ctx.enter_context(nc.Block())

        def sync_part(sp, turn, s, item):
            if item == "xload" and turn.has(item, s):
                if (v := turn.at(lambda n: 2 * (n + 2))) is not None:
                    sp.wait_ge(rows_done, v)
                    sp.sem_inc(passed["sp"], 1)
                b = turn.value(lambda n: n + 2) if turn.register is not None else turn.ns[0] + 2
                src = ids[b] if isinstance(b, int) else ids[bass.ds(b, 1)].rearrange("a p t -> (a p) t")
                sp.dma_start(ids_sb[:], src).then_inc(ids_in, 16)
            elif item in ("sw0", "sw1") and turn.has(item, s):
                c = int(item[-1])
                if (v := turn.at(lambda n: out_of(f"k{c}", n + 1))) is not None:
                    sp.wait_ge(lin_drained[bank_of(f"k{c}")], v)
                    sp.sem_inc(passed["sp"], 1)
                for to, of in ((0, P // 2), (P // 2, 0)):
                    sp.dma_start(swapped[to:to + P // 2, :, :], raw[of:of + P // 2, :, :]).then_inc(swap_in[c], 16)
            elif item[:2] == "st" and turn.has(item, s):
                c, third = int(item[2]), int(item[3])
                off = BATCH[item]
                if (v := turn.at(lambda n: 2 * (KC * (n + off) + c + 1))) is not None:
                    sp.wait_ge(split_lo, v)
                    sp.sem_inc(passed["sp"], 1)
                if (v := turn.at(lambda n: NM * (NG * (n + off - 1) + 2 * c + 2))) is not None:
                    sp.wait_ge(max_full, v)
                    sp.sem_inc(passed["sp"], 1)
                if (v := turn.at(lambda n: NE * (NG * (n + off - 1) + 2 * c + 2))) is not None:
                    sp.wait_ge(exp_full, v)
                    sp.sem_inc(passed["sp"], 1)
                for k in (2 * third, 2 * third + 1):
                    for j, (stack, part) in enumerate(((qs, Q_PART[k]), (ks, K_PART[k]))):
                        sp.dma_start(stack[D * k:D * k + D, HC * c:HC * c + HC, :], parts[part][:, c, j, :]).then_inc(stack_in[c], 16)
            elif item == "mT" and turn.has(item, s):
                g = (s - 1) % NG
                if (v := turn.at(lambda n: out_of("mT", NG * n + s - 1))) is not None:
                    sp.wait_ge(lin_drained[bank_of("mT", s)], v)
                    sp.sem_inc(passed["sp"], 1)
                for j in range(2):
                    sp.dma_start(qs[KS + j:KS + j + 1, HG * g:HG * g + HG, :], maxT[:, g % 2, j, :]).then_inc(max_in[g], 16)
            elif item == "PV3" and turn.has(item, s):
                g = (s - 2) % NG
                c = g // 2
                if (v := turn.at(lambda n: NG * n + s - 2 + 1)) is not None:
                    sp.wait_ge(y_out, v)
                    sp.sem_inc(passed["sp"], 1)
                if (v := turn.at(lambda n: lin("pj1", (NG * n + s - 2) // NG - 2))) is not None:
                    sp.wait_ge(lin_full, v)
                    sp.sem_inc(passed["sp"], 1)
                par = (turn.parity + (s - 2) // NG) % 2
                sp.dma_start(y[par][64 * (g % 2):64 * (g % 2) + 64, c, :], y_raw[0:P:2, :]).then_inc(y_in[g], 16)
                sp.dma_start(sums[:, g, :], y_raw[1:P:32, :]).then_inc(y_in[g], 16)
            elif item == "ro" and turn.has(item, s):
                g = (s - 2) % NG
                if (v := turn.at(lambda n: NG * n + s - 2 + 1)) is not None:
                    sp.wait_ge(inv_done, v)
                    sp.sem_inc(passed["sp"], 1)
                if (v := turn.at(lambda n: 16 * ((NG * n + s - 2) // NG))) is not None:
                    sp.wait_ge(inv_in[g], v)
                    sp.sem_inc(passed["sp"], 1)
                sp.dma_start(inv_dram[g].rearrange("h (q t) -> (h q) t", t=HG * T // P), inv_sums[:, g, :]).then_inc(inv_out[g], 16)
            elif item == "rb" and turn.has(item, s):
                g = (s - 2) % NG
                c = g // 2
                if (v := turn.at(lambda n: 16 * ((NG * n + s - 2) // NG + 1))) is not None:
                    sp.wait_ge(inv_out[g], v)
                    sp.sem_inc(passed["sp"], 1)
                if (v := turn.at(lambda n: KC * ((NG * n + s - 2) // NG - 1) + c + 1)) is not None:
                    sp.wait_ge(y_norm, v)
                    sp.sem_inc(passed["sp"], 1)
                sp.dma_start(inv_rows[64 * (g % 2):64 * (g % 2) + 64, c, :],
                             inv_dram[g].unsqueeze(1).to_broadcast([HG, D, T])).then_inc(inv_in[g], 16)
            elif item == "out" and turn.has(item, s):
                if (v := turn.at(lambda n: 2 * (n - 2 + 1))) is not None:
                    sp.wait_ge(fin_done, v)
                    sp.sem_inc(passed["sp"], 1)
                b = turn.value(lambda n: n - 2) if turn.register is not None else turn.ns[0] - 2
                dst = out[b] if isinstance(b, int) else out[bass.ds(b, 1)].rearrange("a p k c -> (a p) k c")
                sp.dma_start(dst, gate[:]).then_inc(stored, 16)

        @block.sync
        def _(sp):
            loads = [(wtok[:, 0:EC - 1, :], w_tok[0:(EC - 1) * P, :].rearrange("(k p) c -> p k c", p=P)),
                     (wtok[0:EL, EC - 1, :], w_tok[(EC - 1) * P:EW, :]),
                     (stage, w_qkv.rearrange("(k p) c -> p k c", p=P))]
            loads += [(to, of.rearrange("(k p) c -> p k c", p=P)) for to, of in ((wp, w_p), (wr, w_r), (wk, w_k), (wv, w_v))]
            loads += [(bqk[:], b_qk), (bvcol[:], b_v), (bprow[:], b_p), (muc[:], mu), (rope[:], cos_sin), (cst[:], consts)]
            assert len(loads) == NLOADS
            for turn in turns(sp):
                if turn.ns == [FIRST_N + 1]:
                    for to, of in loads:
                        sp.dma_start(to, of).then_inc(s_load, 16)
                for s in range(NG):
                    for item in STEPS[s]:
                        sync_part(sp, turn, s, item)
            sp.wait_ge(stored, 16 * B)

        def lin_unit(pe, turn, s, item):
            key = (lambda n: NG * n + s - 1) if item == "mT" else (lambda n: n + LIN_BATCH[item])
            if (v := turn.at(lambda n: out_of(item, key(n)) - 1)) is not None:
                pe.wait_ge(lin_drained[bank_of(item, s)], v)

        def tensor_part(pe, turn, s, item):
            bank = bank_of(item, s)
            if item[0] == "M":
                k = int(item[1:])
                tb, heads = MAX_TILES[k]
                g = s
                slot = (g + k) % 2
                if k == 0:
                    if (v := turn.at(lambda n: 16 * NSTACK * (n + 1))) is not None:
                        pe.wait_ge(stack_in[g // 2], v)
                if (v := turn.at(lambda n: NM * (NG * n + s) + k - 1)) is not None:
                    pe.wait_ge(max_done, v)
                width = P * (tb + 1)
                tile = ps_max[:, slot, 0:width * len(heads)].rearrange("p (h t) -> p h t", h=len(heads))
                pe.matmul(tile[:, :, P * tb:], ident_bf[:], mask_bf[:].unsqueeze(1).to_broadcast([P, len(heads), P]),
                          start=True, stop=False, skip_group_check=True)
                for j, hd in enumerate(heads):
                    hh = HG * g + hd
                    mm = pe.matmul(tile[:, j, :], qs[0:KS, hh, P * tb:P * tb + P], ks[0:KS, hh, 0:width],
                                   start=False, stop=(j == len(heads) - 1), skip_group_check=True)
                mm.then_inc(max_full, 1)
            elif item[0] == "U":
                k = int(item[1:])
                sbk, heads = EXP_TILES[k]
                g = (s - 1) % NG
                slot = k % EXP_BANKS
                if k == 0:
                    if (v := turn.at(lambda n: 32 * ((NG * n + s - 1) // NG + 1))) is not None:
                        pe.wait_ge(max_in[g], v)
                back = EXP_BANKS if k >= EXP_BANKS else NE - max(m for m in range(NE) if m % EXP_BANKS == slot) + k
                if (v := turn.at(lambda n: NE * (NG * n + s - 1) + k - back + 1)) is not None:
                    pe.wait_ge(exp_done, v)
                width = T - P * sbk
                for j, hd in enumerate(heads):
                    hh = HG * g + hd
                    mm = pe.matmul(ps_exp[:, slot, width * j:width * j + width], ks[:, hh, P * sbk:P * sbk + P],
                                   qs[:, hh, P * sbk:T], start=(j == 0), stop=(j == len(heads) - 1),
                                   skip_group_check=True)
                mm.then_inc(exp_full, 1)
            elif item[0:2] == "PV":
                sbk = int(item[2])
                g = (s + GROUP[item]) % NG
                off = GROUP[item]
                par = (turn.parity + (s + off) // NG) % 2
                if (v := turn.at(lambda n: TB * (NG * n + s + off) + sbk + 1)) is not None:
                    pe.wait_ge(masked, v)
                if sbk == 0:
                    if (v := turn.at(lambda n: NG * n + s + off)) is not None:
                        pe.wait_ge(y_out, v)
                    if (v := turn.at(lambda n: out_of("v1", (NG * n + s + off) // NG))) is not None:
                        pe.wait_ge(lin_drained[bank_of("v1")], v)
                for j in range(HG):
                    hh = HG * g + j
                    mm = pe.matmul(ps_pv[32 * j:32 * j + 32, P * sbk:T],
                                   vx[par][:, sbk, D * hh:D * hh + D, :].rearrange("p d e -> p (d e)"),
                                   probs[sbk][:, j, :], start=(sbk == 0), stop=(sbk == TB - 1), skip_group_check=True)
                mm.then_inc(pv_done, 1)
            elif item == "mT":
                g = (s - 1) % NG
                lin_unit(pe, turn, s, item)
                if (v := turn.at(lambda n: NM * (NG * n + s))) is not None:
                    pe.wait_ge(max_done, v)
                pe.transpose(ps_lin[bank][0:HG * TB, 0:P], rowmax[:, g % 2, :], cst[:, 0, :]).then_inc(lin_full, 1)
            elif item[:2] == "eT":
                c = int(item[2])
                rows = P if c < EC - 1 else EL
                lin_unit(pe, turn, s, item)
                if (v := turn.at(lambda n: 16 * TB * (n + 1 + 1))) is not None:
                    pe.wait_ge(gathered, v)
                for tb in range(TB):
                    mm = pe.transpose(ps_lin[bank][0:rows, P * tb:P * tb + P], emb[:, tb, P * c:P * c + rows], cst[:, 0, :])
                mm.then_inc(lin_full, 1)
            elif item in ("h0", "h1"):
                u = int(item[1])
                lin_unit(pe, turn, s, item)
                if (v := turn.at(lambda n: out_of("eT2", n + 1))) is not None:
                    pe.wait_ge(lin_drained[bank_of("eT2")], v)
                for j in range(2):
                    tb = 2 * u + j
                    for c in range(EC):
                        rows = P if c < EC - 1 else EL
                        mm = pe.matmul(ps_lin[bank][:, C * j:C * j + C], embT[0:rows, c, P * tb:P * tb + P], wtok[0:rows, c, :],
                                       start=(c == 0), stop=(c == EC - 1))
                mm.then_inc(lin_full, 1)
            elif item[:2] == "xT" or item[:3] == "x2T":
                c = int(item[-1])
                first = item[:2] == "xT"
                off = 1 if first else -2
                lin_unit(pe, turn, s, item)
                if (v := turn.at(lambda n: TB * (n + off + 1))) is not None:
                    pe.wait_ge(ln_out[0 if first else 1], v)
                for tb in range(TB):
                    mm = pe.transpose(ps_lin[bank][:, P * tb:P * tb + P], xn[:, tb, P * c:P * c + P], cst[:, 0, :])
                mm.then_inc(lin_full, 1)
            elif item in ("q0", "k0", "q1", "k1"):
                c, col = int(item[1]), C * (item[0] == "k")
                lin_unit(pe, turn, s, item)
                if (v := turn.at(lambda n: out_of("xT1", n + 1))) is not None:
                    pe.wait_ge(lin_drained[bank_of("xT1")], v)
                products = [(w, x, k) for w, x in ((wqkv_hi, xy_hi), (wqkv_hi, xy_lo), (wqkv_lo, xy_hi)) for k in range(KC)]
                for j, (w, x, k) in enumerate(products):
                    mm = pe.matmul(ps_lin[bank][:], w[:, k, col + P * c:col + P * c + P], x[:, k, :],
                                   start=(j == 0), stop=(j == len(products) - 1))
                mm.then_inc(lin_full, 1)
            elif item in ("v0", "v1"):
                u = int(item[1])
                lin_unit(pe, turn, s, item)
                if (v := turn.at(lambda n: out_of("xT1", n + 1))) is not None:
                    pe.wait_ge(lin_drained[bank_of("xT1")], v)
                products = [(w, x, k) for w, x in ((wqkv_hi, xy_hi), (wqkv_hi, xy_lo), (wqkv_lo, xy_hi)) for k in range(KC)]
                for j in range(2):
                    tb = 2 * u + j
                    for m, (w, x, k) in enumerate(products):
                        mm = pe.matmul(ps_lin[bank][:, C * j:C * j + C], x[:, k, P * tb:P * tb + P], w[:, k, 2 * C:3 * C],
                                       start=(m == 0), stop=(m == len(products) - 1))
                mm.then_inc(lin_full, 1)
            elif item in ("pj0", "pj1", "r0", "r1", "kv0", "kv1"):
                u, kind = int(item[-1]), item[:-1]
                x_hi, x_lo, w_hi, w_lo = {"pj": (xy_hi, xy_lo, wp_hi, wp_lo), "r": (mix_hi, mix_lo, wr_hi, wr_lo),
                                          "kv": (mix_hi, mix_lo, wv_hi, wv_lo)}[kind]
                lin_unit(pe, turn, s, item)
                if kind == "pj":
                    if turn.ns == [1]:
                        pe.wait_ge(s_split, 1)
                    if (v := turn.at(lambda n: KC * (n - 1 + 1))) is not None:
                        pe.wait_ge(lo_done["y"], v)
                elif kind == "r":
                    if (v := turn.at(lambda n: KC * (n - 2 + 1))) is not None:
                        pe.wait_ge(lo_done["mr"], v)
                else:
                    if (v := turn.at(lambda n: KC * (n - 2 + 1))) is not None:
                        pe.wait_ge(lo_done["ka"], v)
                products = [(w, x, k) for w, x in ((w_hi, x_hi), (w_lo, x_hi), (w_hi, x_lo)) for k in range(KC)]
                for j in range(2):
                    tb = 2 * u + j
                    for m, (w, x, k) in enumerate(products):
                        mm = pe.matmul(ps_lin[bank][:, C * j:C * j + C], x[:, k, P * tb:P * tb + P], w[:, k, :],
                                       start=(m == 0), stop=(m == len(products) - 1))
                mm.then_inc(lin_full, 1)
            elif item in ("kk0", "kk1"):
                c = int(item[-1])
                lin_unit(pe, turn, s, item)
                if (v := turn.at(lambda n: KC * (n - 2 + 1))) is not None:
                    pe.wait_ge(lo_done["mk"], v)
                products = [(w, x, k) for w, x in ((wk_hi, mix_hi), (wk_lo, mix_hi), (wk_hi, mix_lo)) for k in range(KC)]
                for j, (w, x, k) in enumerate(products):
                    mm = pe.matmul(ps_lin[bank][:], w[:, k, P * c:P * c + P], x[:, k, :],
                                   start=(j == 0), stop=(j == len(products) - 1))
                mm.then_inc(lin_full, 1)

        @block.tensor
        def _(pe):
            pe.wait_ge(s_load, 16 * NLOADS)
            pe.wait_ge(s_setup, SETUP_ONES)
            for k in range(KC):
                pe.matmul(ps_lin[0][:, 0:C], bvcol[:, k:k + 1].to_broadcast([P, P]), wp[:, k, :], start=(k == 0), stop=False)
            pe.matmul(ps_lin[0][:, 0:C], ones_row[:], bprow[:], start=False, stop=True).then_inc(s_bias_mm, 1)
            pe.wait_ge(s_ready, 1)
            for turn in turns(pe):
                for s in range(NG):
                    for item in STEPS[s]:
                        if turn.has(item, s) if item in BATCH or item in GROUP else False:
                            tensor_part(pe, turn, s, item)

        def full(engine, turn, item):
            if (v := turn.at(lambda n: lin(item, n + LIN_BATCH[item]))) is not None:
                engine.wait_ge(lin_full, v)

        def scalar_part(act, turn, s, item):
            bank = bank_of(item, s)
            if item[0] == "U":
                k = int(item[1:])
                sbk, heads = EXP_TILES[k]
                width = len(heads) * (T - P * sbk)
                if (v := turn.at(lambda n: NE * (NG * n + s - 1) + k + 1)) is not None:
                    act.wait_ge(exp_full, v)
                if turn.ns == [0] and s == 1 and k == 0:
                    act.wait_ge(s_split, 1)
                if (v := turn.at(lambda n: TB * (NG * n + s - 1 - 1) + sbk + 1)) is not None:
                    act.wait_ge(pv_done, v)
                act.activation(probs[sbk][:, heads[0]:heads[-1] + 1, :].rearrange("p h t -> p (h t)"),
                               ps_exp[:, k % EXP_BANKS, 0:width], ACT.Exp, scale=SCALE).then_inc(exp_done, 1)
            elif item == "PV3":
                g = (s - 2) % NG
                if (v := turn.at(lambda n: TB * (NG * n + s - 2 + 1))) is not None:
                    act.wait_ge(pv_done, v)
                if (v := turn.at(lambda n: 32 * ((NG * n + s - 2 - 1) // NG + 1))) is not None:
                    act.wait_ge(y_in[(g - 1) % NG], v)
                act.activation(y_raw[:], ps_pv[:], ACT.Copy).then_inc(y_out, 1)
            elif item == "mT":
                g = (s - 1) % NG
                if (v := turn.at(lambda n: lin("mT", NG * n + s - 1))) is not None:
                    act.wait_ge(lin_full, v)
                if (v := turn.at(lambda n: 32 * ((NG * n + s - 1 - 2) // NG + 1))) is not None:
                    act.wait_ge(max_in[(g - 2) % NG], v)
                act.activation(maxT[:, g % 2, 0, :], ps_lin[bank][0:HG * TB, 0:P], ACT.Copy).then_inc(max_hi, 1)
            elif item[:2] == "eT":
                c = int(item[2])
                rows = P if c < EC - 1 else EL
                full(act, turn, item)
                if (v := turn.at(lambda n: lin("h1", n))) is not None:
                    act.wait_ge(lin_full, v)
                act.activation(embT[0:rows, c, :], ps_lin[bank][0:rows, :], ACT.Copy).then_inc(lin_drained[bank], 1)
            elif item[:2] == "xT":
                c = int(item[2])
                full(act, turn, item)
                if (v := turn.at(lambda n: max(lin("k1", n), lin("v1", n), lin("pj1", n - 2)))) is not None:
                    act.wait_ge(lin_full, v)
                act.activation(xy_hi[:, c, :], ps_lin[bank][:], ACT.Copy).then_inc(xT_hi_done, 1)
            elif item in ("q0", "k0", "q1", "k1"):
                c, j = int(item[1]), int(item[0] == "k")
                full(act, turn, item)
                if (v := turn.at(lambda n: 2 * (KC * (n + 1) + c - 1) + j + 1)) is not None:
                    act.wait_ge(split_lo, v)
                act.activation(raw[:, j, :], ps_lin[bank][:], ACT.Identity, bias=bqk[:, 2 * j + c:2 * j + c + 1]).then_inc(lin_drained[bank], 1)
            elif item in ("v0", "v1"):
                u = int(item[1])
                par = (turn.parity + 1) % 2
                full(act, turn, item)
                if (v := turn.at(lambda n: TB * NG * (n + 1 - 2 + 1))) is not None:
                    act.wait_ge(pv_done, v)
                act.activation(vx[par][:, 2 * u:2 * u + 2, :, 0], ps_lin[bank][:].rearrange("p (t c) -> p t c", t=2),
                               ACT.Copy).then_inc(lin_drained[bank], 1)
            elif item[:2] == "hi":
                c, j = int(item[2]), int(item[3])
                if (v := turn.at(lambda n: 2 * (KC * (n + 1) + c) + j + 1)) is not None:
                    act.wait_ge(rope_sum, v)
                if (v := turn.at(lambda n: 16 * NSTACK * (n + 1))) is not None:
                    act.wait_ge(stack_in[c], v)
                act.activation(parts[0][:, c, j, :], raw[:, j, :], ACT.Copy).then_inc(split_hi, 1)
            elif item[:2] == "md":
                c, j = int(item[2]), int(item[3])
                if (v := turn.at(lambda n: 2 * (KC * (n + 1) + c) + j + 1)) is not None:
                    act.wait_ge(split_rest, v)
                act.activation(parts[1][:, c, j, :], raw[:, j, :], ACT.Copy).then_inc(split_mid, 1)
            elif item in ("h0", "h1"):
                u = int(item[1])
                full(act, turn, item)
                if (v := turn.at(lambda n: 2 * (n + 1))) is not None:
                    act.wait_ge(hb_done, v)
                if (v := turn.at(lambda n: TB * (n + 1))) is not None:
                    act.wait_ge(ln_out[0], v)
                act.activation(h[:, 2 * u:2 * u + 2, :], ps_lin[bank][:].rearrange("p (t c) -> p t c", t=2),
                               ACT.Copy).then_inc(lin_drained[bank], 1)
            elif item in ("sq0", "sq1"):
                c = int(item[2])
                if (v := turn.at(lambda n: out_of(f"kk{c}", n - 2))) is not None:
                    act.wait_ge(lin_drained[bank_of(f"kk{c}")], v)
                act.activation(kact[:, c, :], kact[:, c, :], ACT.Square).then_inc(sq_done, 1)
            elif item in ("yh0", "yh1"):
                c = int(item[2])
                if (v := turn.at(lambda n: KC * (n - 1) + c + 1)) is not None:
                    act.wait_ge(y_norm, v)
                if (v := turn.at(lambda n: max(lin("k1", n + 1), lin("v1", n + 1), lin("pj1", n - 2)))) is not None:
                    act.wait_ge(lin_full, v)
                act.activation(xy_hi[:, c, :], y[(turn.parity + 1) % 2][:, c, :], ACT.Copy).then_inc(hi_done["y"], 1)
            elif item in ("mrh0", "mrh1"):
                c = int(item[3])
                if (v := turn.at(lambda n: 2 * (KC * (n - 2) + c) + 1)) is not None:
                    act.wait_ge(mix_step, v)
                if (v := turn.at(lambda n: lin("kv1", n - 3))) is not None:
                    act.wait_ge(lin_full, v)
                act.activation(mix_hi[:, c, :], mix_r[:, c, :], ACT.Copy).then_inc(hi_done["mr"], 1)
            elif item in ("mkh0", "mkh1"):
                c = int(item[3])
                if (v := turn.at(lambda n: 2 * (KC * (n - 2) + c) + 2)) is not None:
                    act.wait_ge(mix_step, v)
                if (v := turn.at(lambda n: lin("r1", n - 2))) is not None:
                    act.wait_ge(lin_full, v)
                act.activation(mix_hi[:, c, :], mix_k[:, c, :], ACT.Copy).then_inc(hi_done["mk"], 1)
            elif item in ("kah0", "kah1"):
                c = int(item[3])
                if (v := turn.at(lambda n: KC * (n - 2) + c + 1)) is not None:
                    act.wait_ge(sq_done, v)
                if (v := turn.at(lambda n: lin("kk1", n - 2))) is not None:
                    act.wait_ge(lin_full, v)
                act.activation(mix_hi[:, c, :], kact[:, c, :], ACT.Copy).then_inc(hi_done["ka"], 1)
            elif item in ("x2T0", "x2T1"):
                c = int(item[3])
                full(act, turn, item)
                if (v := turn.at(lambda n: 2 * KC * (n - 2))) is not None:
                    act.wait_ge(mix_step, v)
                act.activation(x2T[:, c, 1:T + 1], ps_lin[bank][:], ACT.Copy).then_inc(lin_drained[bank], 1)
            elif item in ("kk0", "kk1"):
                c = int(item[2])
                full(act, turn, item)
                if (v := turn.at(lambda n: KC * (n - 2 + 1))) is not None:
                    act.wait_ge(lo_done["mr"], v)
                act.activation(kact[:, c, :], ps_lin[bank][:], ACT.Relu).then_inc(lin_drained[bank], 1)
            elif item in ("r0", "r1"):
                u = int(item[1])
                full(act, turn, item)
                if (v := turn.at(lambda n: 16 * (n - 2))) is not None:
                    act.wait_ge(stored, v)
                act.activation(gate[:, 2 * u:2 * u + 2, :], ps_lin[bank][:].rearrange("p (t c) -> p t c", t=2),
                               ACT.Tanh, scale=0.5).then_inc(lin_drained[bank], 1)

        @block.scalar
        def _(act):
            act.wait_ge(s_load, 16 * NLOADS)
            act.wait_ge(s_ready, 1)
            for turn in turns(act):
                for s in range(NG):
                    for item in STEPS[s]:
                        if turn.has(item, s) if item in BATCH or item in GROUP else False:
                            scalar_part(act, turn, s, item)

        def ln_stats(dve, turn, j, x, off, half, unit):
            if (v := turn.at(lambda n: out_of(unit, n + off))) is not None:
                dve.wait_ge(lin_drained[bank_of(unit)], v)
            for tb in (2 * half, 2 * half + 1):
                dve.bn_stats(ln[j]["stats"][:, tb, :], x[:, tb, :]).then_inc(ln_step[j], 1)

        def ln_variance(dve, turn, j, off):
            a = ln[j]
            if (v := turn.at(lambda n: 9 * (n + off) + TB)) is not None:
                dve.wait_ge(ln_step[j], v)
                dve.sem_inc(passed["dve"], 1)
            if (v := turn.at(lambda n: TB * (n + off))) is not None:
                dve.wait_ge(ln_out[j], v)
                dve.sem_inc(passed["dve"], 1)
            for tb in range(TB):
                dve.bn_aggr(a["mv"][:, tb, :], a["stats"][:, tb, :]).then_inc(ln_step[j], 1)
            if (v := turn.at(lambda n: 9 * (n + off) + 2 * TB)) is not None:
                dve.wait_ge(ln_step[j], v)
            dve.tensor_scalar(a["var"][:], a["mv"][:, :, 1], EPS, None, ALU.add).then_inc(ln_step[j], 1)

        def ln_normalise(dve, turn, j, x, off, half, before):
            a = ln[j]
            if (v := turn.at(lambda n: n + off + 1)) is not None:
                dve.wait_ge(ln_rstd[j], v)
            if (v := turn.at(before)) is not None:
                dve.wait_ge(lin_full, v)
            for tb in (2 * half, 2 * half + 1):
                dve.tensor_scalar(xn[:, tb, :], x[:, tb, :], a["mv"][:, tb, 0:1], a["rstd"][:, tb:tb + 1],
                                  ALU.subtract, ALU.mult).then_inc(ln_out[j], 1)

        def vector_part(dve, turn, s, item):
            bank = bank_of(item, s)
            if item[0] == "M":
                k = int(item[1:])
                tb, heads = MAX_TILES[k]
                slot = (s + k) % 2
                width = P * (tb + 1)
                if (v := turn.at(lambda n: NM * (NG * n + s) + k + 1)) is not None:
                    dve.wait_ge(max_full, v)
                src = ps_max[:, slot, 0:width * len(heads)].rearrange("p (h t) -> p h t", h=len(heads))
                dst = rowmax[:, s % 2, :].rearrange("p (h t) -> p h t", h=HG)[:, heads[0]:heads[-1] + 1, tb]
                dve.tensor_reduce(dst, src, AX.X, ALU.max).then_inc(max_done, 1)
            elif item == "mT":
                g = (s - 1) % NG
                if (v := turn.at(lambda n: NG * n + s - 1 + 1)) is not None:
                    dve.wait_ge(max_hi, v)
                dve.tensor_tensor(maxT[:, g % 2, 1, :], ps_lin[bank][0:HG * TB, 0:P], maxT[:, g % 2, 0, :],
                                  ALU.subtract).then_inc(lin_drained[bank], 1)
            elif item == "idx":
                if (v := turn.at(lambda n: 16 * (n + 2 + 1))) is not None:
                    dve.wait_ge(ids_in, v)
                dve.tensor_scalar(row_t[:], ids_sb[:], 1.0, 0.0, ALU.add, ALU.max).then_inc(rows_done, 1)
                if (v := turn.at(lambda n: 2 * (n + 2) + 1)) is not None:
                    dve.wait_ge(rows_done, v)
                if (v := turn.at(lambda n: 16 * TB * (n + 2))) is not None:
                    dve.wait_ge(gathered, v)
                dve.tensor_scalar(row_id[:], row_t[:], float(ROWS + 1), None, ALU.min).then_inc(rows_done, 1)
            elif item in ("ln1a0", "ln1a1"):
                ln_stats(dve, turn, 0, h, 1, int(item[-1]), f"h{item[-1]}")
            elif item == "ln1v":
                ln_variance(dve, turn, 0, 1)
            elif item in ("ln1n0", "ln1n1"):
                ln_normalise(dve, turn, 0, h, 1, int(item[-1]), lambda n: max(lin("x2T1", n - 2), lin("xT1", n)))
            elif item in ("ln2a0", "ln2a1"):
                ln_stats(dve, turn, 1, h1, -1, int(item[-1]), f"pj{item[-1]}")
            elif item == "ln2v":
                ln_variance(dve, turn, 1, -1)
            elif item in ("ln2n0", "ln2n1"):
                ln_normalise(dve, turn, 1, h1, -1, int(item[-1]), lambda n: max(lin("xT1", n + 1), lin("x2T1", n - 2)))
            elif item in ("xT0", "xT1"):
                c = int(item[2])
                if (v := turn.at(lambda n: KC * (n + 1) + c + 1)) is not None:
                    dve.wait_ge(xT_hi_done, v)
                dve.tensor_tensor(xy_lo[:, c, :], ps_lin[bank][:], xy_hi[:, c, :].bitcast(F32), ALU.subtract).then_inc(lin_drained[bank], 1)
            elif item[:2] == "tt":
                c, j = int(item[2]), int(item[3])
                if (v := turn.at(lambda n: 2 * (KC * (n + 1) + c) + j + 1)) is not None:
                    dve.wait_ge(split_hi, v)
                dve.tensor_tensor(raw[:, j, :], raw[:, j, :], parts[0][:, c, j, :], ALU.subtract).then_inc(split_rest, 1)
            elif item[:2] == "lo":
                c, j = int(item[2]), int(item[3])
                if (v := turn.at(lambda n: 2 * (KC * (n + 1) + c) + j + 1)) is not None:
                    dve.wait_ge(split_mid, v)
                dve.tensor_tensor(parts[2][:, c, j, :], raw[:, j, :], parts[1][:, c, j, :], ALU.subtract).then_inc(split_lo, 1)
            elif item == "rc":
                g = (s - 2) % NG
                if (v := turn.at(lambda n: 32 * ((NG * n + s - 2) // NG + 1))) is not None:
                    dve.wait_ge(y_in[g], v)
                if (v := turn.at(lambda n: 16 * ((NG * n + s - 2) // NG))) is not None:
                    dve.wait_ge(inv_out[g], v)
                dve.reciprocal(inv_sums[:, g, :], sums[:, g, :]).then_inc(inv_done, 1)
            elif item in ("yn0", "yn1"):
                c = int(item[2])
                for g in (2 * c, 2 * c + 1):
                    if (v := turn.at(lambda n: 32 * (n - 1 + 1))) is not None:
                        dve.wait_ge(y_in[g], v)
                    if (v := turn.at(lambda n: 16 * (n - 1 + 1))) is not None:
                        dve.wait_ge(inv_in[g], v)
                yb = y[(turn.parity + 1) % 2][:, c, :]
                dve.tensor_tensor(yb, yb, inv_rows[:, c, :], ALU.mult).then_inc(y_norm, 1)
            elif item in ("pj0", "pj1"):
                u = int(item[2])
                par = (turn.parity + 1) % 2
                full(dve, turn, item)
                if (v := turn.at(lambda n: 2 * (n - 1 + 1))) is not None:
                    dve.wait_ge(hb_done, v)
                if (v := turn.at(lambda n: TB * (n - 1))) is not None:
                    dve.wait_ge(ln_out[1], v)
                if (v := turn.at(lambda n: 2 * (n - 1))) is not None:
                    dve.wait_ge(fin_done, v)
                dve.tensor_tensor(h1[:, 2 * u:2 * u + 2, :], ps_lin[bank][:].rearrange("p (t c) -> p t c", t=2),
                                  hb[par][:, 2 * u:2 * u + 2, :], ALU.add).then_inc(lin_drained[bank], 1)
            elif item in ("mm0", "mm1"):
                c = int(item[2])
                before = x2T[:, c, 0:T]
                if (v := turn.at(lambda n: KC * (n - 2) + c + 1)) is not None:
                    dve.wait_ge(mix_diff, v)
                if (v := turn.at(lambda n: KC * (n - 2))) is not None:
                    dve.wait_ge(lo_done["ka"], v)
                dve.scalar_tensor_tensor(out=mix_r[:, c, :], in0=mix_k[:, c, :], scalar=muc[:, 0, c:c + 1], in1=before,
                                         op0=ALU.mult, op1=ALU.add).then_inc(mix_step, 1)
                if (v := turn.at(lambda n: 2 * (KC * (n - 2) + c) + 1)) is not None:
                    dve.wait_ge(mix_step, v)
                dve.scalar_tensor_tensor(out=mix_k[:, c, :], in0=mix_k[:, c, :], scalar=muc[:, 1, c:c + 1], in1=before,
                                         op0=ALU.mult, op1=ALU.add).then_inc(mix_step, 1)
            elif item in ("kv0", "kv1"):
                u = int(item[2])
                full(dve, turn, item)
                if (v := turn.at(lambda n: out_of("r1", n - 2))) is not None:
                    dve.wait_ge(lin_drained[bank_of("r1")], v)
                half = gate[:, 2 * u:2 * u + 2, :]
                dve.scalar_tensor_tensor(out=half, in0=half, scalar=1.0, in1=ps_lin[bank][:].rearrange("p (t c) -> p t c", t=2),
                                         op0=ALU.add, op1=ALU.mult).then_inc(lin_drained[bank], 1)
            elif item in ("fin0", "fin1"):
                u = int(item[3])
                if (v := turn.at(lambda n: out_of(f"kv{u}", n - 2))) is not None:
                    dve.wait_ge(lin_drained[bank_of(f"kv{u}")], v)
                half = gate[:, 2 * u:2 * u + 2, :]
                dve.scalar_tensor_tensor(out=half, in0=half, scalar=0.5, in1=h1[:, 2 * u:2 * u + 2, :], op0=ALU.mult,
                                         op1=ALU.add).then_inc(fin_done, 1)

        def prepare(dve):
            dve.wait_ge(s_load, 16 * NLOADS)
            dve.tensor_copy(ident_bf[:], cst[:, 0, :])
            dve.tensor_copy(mask_bf[:], cst[:, 1, :])
            dve.tensor_copy(wqkv_hi[:], stage).then_inc(s_setup, 1)
            dve.wait_ge(s_setup, 2)
            dve.tensor_tensor(wqkv_lo[:], stage, wqkv_hi[:].bitcast(F32), ALU.subtract)
            dve.wait_ge(s_bias_mm, 1)
            dve.tensor_copy(bias_p[:], ps_lin[0][:, 0:C]).then_inc(s_ready, 1)
            for hi, w in ((wp_hi, wp), (wr_hi, wr), (wk_hi, wk), (wv_hi, wv)):
                dve.tensor_copy(hi[:], w).then_inc(s_split_hi, 1)
            dve.wait_ge(s_split_hi, 4)
            for hi, lo, w in ((wp_hi, wp_lo, wp), (wr_hi, wr_lo, wr), (wk_hi, wk_lo, wk), (wv_hi, wv_lo, wv)):
                last = dve.tensor_tensor(lo[:], w, hi[:].bitcast(F32), ALU.subtract)
            last.then_inc(s_split, 1)

        @block.vector
        def _(dve):
            dve.memset(ones_row[:], 1.0).then_inc(s_setup, 1)
            dve.memset(minus_half[:], -0.5)
            for v in vx:
                dve.memset(v[:, :, :, 1], 1.0)
            dve.memset(x2T[:, :, 0:1], 0.0)
            dve.memset(ks[KS:KM, :, :], -1.0)
            for turn in turns(dve):
                if turn.ns == [FIRST_N + 1]:
                    prepare(dve)
                for s in range(NG):
                    for item in STEPS[s]:
                        if turn.has(item, s) if item in BATCH or item in GROUP else False:
                            vector_part(dve, turn, s, item)

        def gpsimd_part(pool, turn, s, item):
            if item[0] == "U":
                k = int(item[1:])
                if k + 1 not in EXP_TILES_UPTO:
                    return
                sbk = EXP_TILES_UPTO.index(k + 1)
                if (v := turn.at(lambda n: NE * (NG * n + s - 1) + k + 1)) is not None:
                    pool.wait_ge(exp_done, v)
                    pool.sem_inc(passed["pool"], 1)
                diag = probs[sbk][:, :, 0:P]
                pool.affine_select(out=diag, in_=diag, compare_op=ALU.is_ge, fill=0.0, base=0,
                                   pattern=[[0, HG], [1, P]], channel_multiplier=-1).then_inc(masked, 1)
            elif item == "gather":
                if (v := turn.at(lambda n: 2 * (n + 2 + 1))) is not None:
                    pool.wait_ge(rows_done, v)
                if (v := turn.at(lambda n: lin("eT2", n + 1))) is not None:
                    pool.wait_ge(lin_full, v)
                    pool.sem_inc(passed["pool"], 1)
                for tb in range(TB):
                    pool.indirect_dma_start(out=emb[:, tb, :], out_offset=None, in_=table,
                                            in_offset=bass.IndirectOffsetOnAxis(ap=row_id[:, tb:tb + 1], axis=0)
                                            ).then_inc(gathered, 16)
            elif item in ("ln1p", "ln2p"):
                j = int(item[2]) - 1
                off = BATCH[item]
                if (v := turn.at(lambda n: 9 * (n + off + 1))) is not None:
                    pool.wait_ge(ln_step[j], v)
                if (v := turn.at(lambda n: TB * (n + off))) is not None:
                    pool.wait_ge(ln_out[j], v)
                pool.tensor_tensor(ln[j]["rstd"][:], ln[j]["var"][:], minus_half[:], ALU.pow).then_inc(ln_rstd[j], 1)
            elif item[:-1] in ("yl", "mrl", "mkl", "kal"):
                c, name = int(item[-1]), item[:-2]
                off = BATCH[item]
                high, low = (xy_hi, xy_lo) if name == "y" else (mix_hi, mix_lo)
                whole = {"y": y[(turn.parity + 1) % 2], "mr": mix_r, "mk": mix_k, "ka": kact}[name]
                if (v := turn.at(lambda n: KC * (n + off) + c + 1)) is not None:
                    pool.wait_ge(hi_done[name], v)
                pool.tensor_tensor(low[:, c, :], whole[:, c, :], high[:, c, :].bitcast(F32),
                                   ALU.subtract).then_inc(lo_done[name], 1)
            elif item[:4] == "rcos":
                c, j = int(item[4]), int(item[5])
                if (v := turn.at(lambda n: 32 * (n + 1 + 1))) is not None:
                    pool.wait_ge(swap_in[c], v)
                pool.tensor_tensor(raw[:, j, :], raw[:, j, :], rope[:, 0, :], ALU.mult).then_inc(rope_cos, 1)
            elif item[:4] == "rsin":
                c, j = int(item[4]), int(item[5])
                if (v := turn.at(lambda n: 32 * (n + 1 + 1))) is not None:
                    pool.wait_ge(swap_in[c], v)
                pool.tensor_tensor(swapped[:, j, :], swapped[:, j, :], rope[:, 1, :], ALU.mult).then_inc(rope_sin, 1)
            elif item[:4] == "radd":
                c, j = int(item[4]), int(item[5])
                if (v := turn.at(lambda n: 2 * (KC * (n + 1) + c) + j + 1)) is not None:
                    pool.wait_ge(rope_cos, v)
                if (v := turn.at(lambda n: 2 * (KC * (n + 1) + c) + j + 1)) is not None:
                    pool.wait_ge(rope_sin, v)
                pool.tensor_tensor(raw[:, j, :], raw[:, j, :], swapped[:, j, :], ALU.add).then_inc(rope_sum, 1)
            elif item in ("mix0", "mix1"):
                c = int(item[3])
                x, before = x2T[:, c, 1:T + 1], x2T[:, c, 0:T]
                if (v := turn.at(lambda n: out_of(f"x2T{c}", n - 2))) is not None:
                    pool.wait_ge(lin_drained[bank_of(f"x2T{c}")], v)
                if (v := turn.at(lambda n: KC * (n - 2))) is not None:
                    pool.wait_ge(lo_done["mk"], v)
                pool.tensor_tensor(mix_k[:, c, :], x, before, ALU.subtract).then_inc(mix_diff, 1)
            elif item in ("hb0", "hb1"):
                u = int(item[2])
                par = (turn.parity + 1) % 2
                if (v := turn.at(lambda n: out_of(f"h{u}", n + 1))) is not None:
                    pool.wait_ge(lin_drained[bank_of(f"h{u}")], v)
                if (v := turn.at(lambda n: out_of("pj1", n - 1))) is not None:
                    pool.wait_ge(lin_drained[bank_of("pj1")], v)
                pool.tensor_tensor(hb[par][:, 2 * u:2 * u + 2, :], h[:, 2 * u:2 * u + 2, :],
                                   bias_p[:].unsqueeze(1).to_broadcast([P, 2, C]), ALU.add).then_inc(hb_done, 1)

        @block.gpsimd
        def _(pool):
            for turn in turns(pool):
                if turn.ns == [FIRST_N + 1]:
                    pool.wait_ge(s_load, 16 * NLOADS)
                    pool.wait_ge(s_ready, 1)
                for s in range(NG):
                    for item in STEPS[s]:
                        if turn.has(item, s) if item in BATCH or item in GROUP else False:
                            gpsimd_part(pool, turn, s, item)

def kernel(**inputs):
    import concourse.bacc as bacc
    from concourse.bass_utils import run_bass_kernel_spmd

    def arr(name):
        return np.ascontiguousarray(inputs[name])

    f = np.float32
    ids = np.ascontiguousarray(arr("x").reshape(B, TB, P).transpose(0, 2, 1))
    t0, t1, t2 = arr("L0_tok_t0"), arr("L0_tok_t1"), arr("L0_tok_t2")
    table = np.zeros((ROWS + 2, EW), f)
    r1, r2 = 1 + len(t0), 1 + len(t0) + len(t1)
    table[1:r1, 0:E0] = t0
    table[r1:r2, E0:E0 + E1] = t1
    table[r2:r2 + len(t2), E0 + E1:EW] = t2
    w_tok = np.concatenate([arr("L0_tok_w0"), arr("L0_tok_w1"), arr("L0_tok_w2")], axis=0)
    order = np.arange(C).reshape(KC, HC, D).transpose(0, 2, 1).reshape(-1)
    w_qkv = np.concatenate([arr("L0_attn_wq").T[:, order], arr("L0_attn_wk").T[:, order], arr("L0_attn_wv").T], axis=1)
    b_qk = np.concatenate([arr("L0_attn_bq")[order].reshape(KC, P), arr("L0_attn_bk")[order].reshape(KC, P)]).T
    b_v = arr("L0_attn_bv").reshape(KC, P).T
    mu = np.stack([arr("L0_ffn_mu_r").reshape(KC, P).T, arr("L0_ffn_mu_k").reshape(KC, P).T], axis=1)
    half = D // 2
    i = np.arange(half, dtype=f)
    alpha = (f(1.0) / np.power(f(10000.0), f(2.0) * i / f(D))).astype(f)
    ang = (np.arange(T, dtype=f)[:, None] * alpha).astype(f)
    d_of = np.arange(P) // HC
    cos = np.cos(ang).astype(f).T[d_of % half]
    sin = np.sin(ang).astype(f).T[d_of % half] * np.where(d_of < half, f(-1), f(1))[:, None]
    cos_sin = np.stack([cos, sin], axis=1).astype(f)
    consts = np.stack([np.eye(P, dtype=f), np.triu(np.full((P, P), MASKED, f), 1)], axis=1)
    arrays = dict(ids=ids, table=table, w_tok=w_tok, w_qkv=w_qkv, b_qk=b_qk, w_p=arr("L0_attn_wp").T, b_v=b_v,
                  b_p=arr("L0_attn_bp").reshape(1, C), w_r=arr("L0_ffn_W_r").T, w_k=arr("L0_ffn_W_k").T,
                  w_v=arr("L0_ffn_W_v").T, mu=mu, cos_sin=cos_sin, consts=consts)
    arrays = {name: np.ascontiguousarray(a) for name, a in arrays.items()}

    nc = bacc.Bacc("TRN2", target_bir_lowering=False, num_devices=1)
    args = {name: nc.dram_tensor(f"in_{name}", a.shape, mybir.dt.from_np(a.dtype), kind="ExternalInput").ap()
            for name, a in arrays.items()}
    out = nc.dram_tensor("out_h", (B, T, C), F32, kind="ExternalOutput").ap()
    tower(nc, out=out.rearrange("b (k p) c -> b p k c", p=P), **args)
    r = run_bass_kernel_spmd(nc, [{f"in_{name}": a for name, a in arrays.items()}], core_ids=[0])
    return r.results[0]["out_h"]
```
